# Optimizing a Trainium2 kernel written in Bass

```python
import numpy as np
import jax
import jax.numpy as jnp

def _softmax(x, axis=-1):
    return jax.nn.softmax(x, axis=axis)

def _gelu(x):
    return jax.nn.gelu(x, approximate=True)

def _silu(x):
    return jax.nn.silu(x)

def _sigmoid(x):
    return jax.nn.sigmoid(x)

def _layernorm(x, axis=-1, eps=1e-05):
    m = jnp.mean(x, axis=axis, keepdims=True)
    v = jnp.var(x, axis=axis, keepdims=True)
    return (x - m) / jnp.sqrt(v + eps)

def _scatter_add(tgt, idx, src, axis=0):
    return tgt.at[idx].add(src)

def _segment_sum(src, seg, n):
    return jax.ops.segment_sum(src, seg, n)
kernel_name = 'mk_gnn_ffn_d1_gnn_r8_03ea4a'

def setup_inputs(seed: int=0):
    np.random.seed(seed)
    _w = jnp.asarray

    def _rec_inputs():
        import jax
        import jax.numpy as jnp
        _gk = jax.random.key(seed)
        x = -0.0003019 + 1 * jax.random.normal(jax.random.fold_in(_gk, 1), (1250, 1024), jnp.float32)
        src = jax.random.randint(jax.random.fold_in(_gk, 2), (20000,), 0, 1250, jnp.int32)
        dst = jax.random.randint(jax.random.fold_in(_gk, 3), (20000,), 0, 1250, jnp.int32)
        _o = jnp.argsort(dst, stable=True)
        src = src[_o]
        dst = dst[_o]
        return (x, src, dst)
    x, src, dst = _rec_inputs()

    def _L0_gnn_setup():
        import jax, jax.numpy as jnp
        import numpy as np
        N = 2500
        E = 40000
        D_IN = 1024
        D_OUT = 1024
        key = jax.random.key(seed)
        k1, k2, k3, k4 = jax.random.split(key, 4)
        x = jax.random.normal(k1, (N, D_IN), dtype=jnp.float32)
        edge_index = jax.random.randint(k2, (2, E), 0, N, dtype=jnp.int64)
        W = jax.random.normal(k3, (D_OUT, D_IN), dtype=jnp.float32) * (1.0 / np.sqrt(D_IN))
        b = jax.random.normal(k4, (D_OUT,), dtype=jnp.float32) * 0.01
        return {'x': x, 'edge_index': edge_index, 'W': W, 'b': b}
    _L0_gnn_all = _L0_gnn_setup()
    _L0_gnn_in = {k: v for k, v in _L0_gnn_all.items() if k in ('W', 'b')}
    del _L0_gnn_all

    def _L0_ffn_setup():
        import jax, jax.numpy as jnp
        import numpy as np
        B, S, H = (8, 1024, 1024)
        FF = 512
        E = 8
        TOP_K = 2
        LN_EPS = 1e-12

        def _layernorm(x, w, b):
            mu = jnp.mean(x, axis=-1, keepdims=True)
            var = jnp.mean(jnp.square(x - mu), axis=-1, keepdims=True)
            return (x - mu) * jax.lax.rsqrt(var + LN_EPS) * w + b
        key = jax.random.key(seed)
        ks = jax.random.split(key, 8)
        sc_h = 1.0 / np.sqrt(H)
        sc_ff = 1.0 / np.sqrt(FF)
        return {'hidden_states': jax.random.normal(ks[0], (B, S, H), jnp.float32), 'router_w': jax.random.normal(ks[1], (E, H), jnp.float32) * sc_h, 'router_b': jnp.zeros((E,), jnp.float32), 'w1': jax.random.normal(ks[2], (E, FF, H), jnp.float32) * sc_h, 'b1': jax.random.normal(ks[3], (E, FF), jnp.float32) * 0.01, 'w2': jax.random.normal(ks[4], (E, H, FF), jnp.float32) * sc_ff, 'b2': jax.random.normal(ks[5], (E, H), jnp.float32) * 0.01, 'ln_w': jnp.ones((H,), jnp.float32), 'ln_b': jnp.zeros((H,), jnp.float32)}
    _L0_ffn_all = _L0_ffn_setup()
    _L0_ffn_in = {k: v for k, v in _L0_ffn_all.items() if k in ('router_w', 'router_b', 'w1', 'b1', 'w2', 'b2', 'ln_w', 'ln_b')}
    del _L0_ffn_all
    return {'x': x, 'src': src, 'dst': dst, 'L0_gnn_W': _L0_gnn_in['W'], 'L0_gnn_b': _L0_gnn_in['b'], 'L0_ffn_router_w': _L0_ffn_in['router_w'], 'L0_ffn_router_b': _L0_ffn_in['router_b'], 'L0_ffn_w1': _L0_ffn_in['w1'], 'L0_ffn_b1': _L0_ffn_in['b1'], 'L0_ffn_w2': _L0_ffn_in['w2'], 'L0_ffn_b2': _L0_ffn_in['b2'], 'L0_ffn_ln_w': _L0_ffn_in['ln_w'], 'L0_ffn_ln_b': _L0_ffn_in['ln_b']}

def reference(x, src, dst, L0_gnn_W, L0_gnn_b, L0_ffn_router_w, L0_ffn_router_b, L0_ffn_w1, L0_ffn_b1, L0_ffn_w2, L0_ffn_b2, L0_ffn_ln_w, L0_ffn_ln_b):
    import jax
    import jax.numpy as jnp

    def _L0_gnn_ref(x, edge_index, W, b):
        import jax, jax.numpy as jnp
        import numpy as np
        N = 2500
        E = 40000
        D_IN = 1024
        D_OUT = 1024
        num_nodes = x.shape[0]
        self_idx = jnp.arange(num_nodes, dtype=edge_index.dtype)
        ei = jnp.concatenate([edge_index, jnp.stack([self_idx, self_idx], axis=0)], axis=1)
        row, col = (ei[0], ei[1])
        h = jnp.einsum('nd,od->no', x, W) + b
        deg = jnp.zeros((num_nodes,), dtype=h.dtype).at[row].add(1.0)
        deg_inv_sqrt = deg ** (-0.5)
        norm = deg_inv_sqrt[row] * deg_inv_sqrt[col]
        msg = norm[:, None] * h[col]
        out = jax.ops.segment_sum(msg, row, num_segments=num_nodes)
        return out

    def _L0_ffn_ref(hidden_states, router_w, router_b, w1, b1, w2, b2, ln_w, ln_b):
        import jax, jax.numpy as jnp
        import numpy as np
        B, S, H = (8, 1024, 1024)
        FF = 512
        E = 8
        TOP_K = 2
        LN_EPS = 1e-12

        def _layernorm(x, w, b):
            mu = jnp.mean(x, axis=-1, keepdims=True)
            var = jnp.mean(jnp.square(x - mu), axis=-1, keepdims=True)
            return (x - mu) * jax.lax.rsqrt(var + LN_EPS) * w + b
        b, s, h = hidden_states.shape
        flat = hidden_states.reshape(-1, h)
        logits = flat @ router_w.T + router_b
        topk_vals, topk_idx = jax.lax.top_k(logits, TOP_K)
        topk_w = jax.nn.softmax(topk_vals, axis=-1)
        out = jnp.zeros_like(flat)
        n_exp = w1.shape[0]
        for e in range(n_exp):
            cw = jnp.sum(jnp.where(topk_idx == e, topk_w, 0.0), axis=-1)
            y = jax.nn.gelu(flat @ w1[e].T + b1[e], approximate=False)
            y = y @ w2[e].T + b2[e]
            out = out + y * cw[:, None]
        out = out.reshape(b, s, h) + hidden_states
        return _layernorm(out, ln_w, ln_b)
    edge_index = jnp.stack([src, dst])
    x = x + _L0_gnn_ref(_layernorm(x, axis=-1), edge_index, L0_gnn_W, L0_gnn_b)
    x = x + _L0_ffn_ref(_layernorm(x, axis=-1)[None], L0_ffn_router_w, L0_ffn_router_b, L0_ffn_w1, L0_ffn_b1, L0_ffn_w2, L0_ffn_b2, L0_ffn_ln_w, L0_ffn_ln_b)[0]
    return x

_drawn_inputs = setup_inputs


def setup_inputs(seed=0):
    import zlib

    import numpy as np

    out = dict(_drawn_inputs(seed))
    spreads = {'L0_ffn_router_b': (0.0, 0.1), 'L0_ffn_ln_w': (1.0, 0.2), 'L0_ffn_ln_b': (0.0, 0.1)}
    factors = {'L0_gnn_b': 2.852, 'L0_ffn_b1': 24.252, 'L0_ffn_b2': 8.0}
    for name, (base, spread) in spreads.items():
        noise = np.random.default_rng([zlib.crc32(name.encode()), seed]).standard_normal(out[name].shape)
        drawn = base * np.exp(spread * noise) if base else spread * noise
        out[name] = jnp.asarray(drawn.astype(out[name].dtype))
    for name, factor in factors.items():
        out[name] = (out[name] * factor).astype(out[name].dtype)
    return out
```

```python
from contextlib import ExitStack

import concourse.bass as bass
from concourse import mybir
from concourse.alu_op_type import AluOpType as ALU

F32 = mybir.dt.float32
F16 = mybir.dt.float16
F8 = mybir.dt.float8e4
I32 = mybir.dt.int32
U32 = mybir.dt.uint32
ACT = mybir.ActivationFunctionType
AXX = mybir.AxisListType.X
ds = bass.ds

P = 128
N = 1250
NT = -(-N // P)
NP = NT * P
D = 1024
DK = D // P
HALF = 512
E = 20000
EP = 125
ET = E // EP
BIG = 1000.0
NE = 8
FF = 512
FK = FF // P
PIECES = 8
STAGES = 4
GROUP = 9
SUB = 3
ETP = ET + GROUP
NSTEP = -(-ET // GROUP)
OHW = NP + P
WSCALE = 256.0
EPS1 = 1e-5
EPS2 = 1e-12
CT = 3
CH = CT * P
CPE = -(-N // CH)
CAP = CPE * CH
NROW = NP + CH
XW = D + NE
MAXC = NE + 2 * N // CH + 2
EXACT16 = 2048.0
RANGE_CONSTS, PE_CONSTS, EDGE_CONSTS, ALL_CONSTS = 4, 7, 8, 16
LAST_GROUPS = ((0, 1), (2, 3, 4), (5, 6, 7), (8, 9))
POOL_TILES = 5
EARLY = 4
W2AT = DK * FF


class Steps:

    def __init__(self, eng, sem):
        self.eng, self.sem, self.base, self.k = eng, sem, 0, 0

    def enter(self, base):
        self.base, self.k = base, 0

    def did(self, ins):
        self.k += 1
        ins.then_inc(self.sem, 1)

    def wait(self):
        self.eng.wait_ge(self.sem, self.base + self.k)

    def link(self, ins):
        self.did(ins)
        self.wait()


def build(nc, x, src, dst, dst_rows, wst, b, router_w, router_b, b1, b2, ln_w, ln_b,
          x2_rows, acc_rows, slot_table, out):
    ctx = ExitStack()
    with ctx:
        def sb(name, shape, dt):
            return ctx.enter_context(nc.sbuf_tensor(name, shape, dt))

        def sem(name):
            return ctx.enter_context(nc.semaphore(name))

        early = sb("early", [P, CT * XW], F32)
        iota16 = early[:, 0:NP // 2].bitcast(F16)
        at = NP // 2
        eye_wide = early[:, at:at + NP - P // 2].bitcast(F16)
        zeros16 = eye_wide[:, 0:P]
        at += NP - P // 2
        ct_lo_16 = early[:, at:at + NP // 2].bitcast(F16)
        at += NP // 2
        ct_lo_8 = early[:, at:at + NP // 4].bitcast(F8)
        assert at + NP // 4 <= CT * XW
        gx0 = [early[:, i * XW:(i + 1) * XW] for i in range(CT)]
        ident = sb("ident", [P, P], F32)
        ident16 = sb("ident16", [P, P], F16)
        ones16 = sb("ones16", [P, P], F16)
        tri = sb("tri", [P, NT], F32)
        tri16 = sb("tri16", [P, P], F16)
        block_lo = sb("block_lo", [P, NT], F32)
        block_hi = sb("block_hi", [P, NT], F32)
        tile_no = sb("tile_no", [P, 2], F32)
        b_row = sb("b_row", [P, D], F32)
        src_i = sb("src_i", [EP, ET], I32)
        dst_i = sb("dst_i", [EP, ET], I32)
        src_f = sb("src_f", [EP, ETP], F32)
        dst_f = sb("dst_f", [EP, ETP], F32)
        step_from = sb("step_from", [P, NSTEP], F32)
        steps_in = sb("steps_in", [P, NSTEP], F32)
        tile_min = sb("tile_min", [P, 2], F32)
        tile_max = sb("tile_max", [P, 2], F32)
        overlap = sb("overlap", [P, 2, 16], F32)
        tile_from = sb("tile_from", [P, 2], F32)
        tile_to = sb("tile_to", [P, 2], F32)
        span = sb("span", [P, 8], F32)
        span_row = sb("span_row", [1, 64], F32)
        ranges = sb("ranges", [1, 3, 16], I32)
        t = sb("t", [P, NT * D], F32)
        stage = sb("stage", [P, STAGES * D], F32)
        wbuf0 = sb("wbuf0", [P, 2 * PIECES * D], F16)
        wbuf1 = sb("wbuf1", [P, 2 * NT * D], F16)
        counts = sb("counts", [P, NT * NP * 3 // 4], F32)
        ct_hi = counts[:, 0:NT * NP // 2].bitcast(F16)
        ct_lo = counts[:, NT * NP // 2:].bitcast(F8)
        work = sb("work", [P, CT * D], F32)
        xn = work[:, 0:D]
        x2t = work[:, D:2 * D].bitcast(F16)
        xs = work[:, 2 * D:3 * D].bitcast(F16)
        first_v = work[:, D:D + 2 * P].rearrange("p (h k) -> p h k", h=2)
        last_v = work[:, D + 2 * P:D + 4 * P].rearrange("p (h k) -> p h k", h=2)
        at = D + 4 * P
        dst_r = work[:, at:at + 2 * EP].bitcast(I32).rearrange("p (h k) -> p h k", h=2)
        at += 2 * EP
        dst_rf = work[:, at:at + 2 * EP].rearrange("p (h k) -> p h k", h=2)
        assert at + 2 * EP <= 2 * D
        stats = sb("stats", [P, 12], F32)
        mv = sb("mv", [P, 2], F32)
        std = sb("std", [P, 2], F32)
        rstd = sb("rstd", [P, 1], F32)
        q_col = sb("q_col", [P, 1], F32)
        deg_s = sb("deg_s", [P, NT], F32)
        deg_f = sb("deg_f", [P, NT], F32)
        q_dis = sb("q_dis", [P, NT], F32)
        dis = sb("dis", [P, NT], F32)
        over = sb("over", [P, NT], F16)
        over_row = sb("over_row", [1, 4], F32)
        over_i = sb("over_i", [1, 4], I32)
        hold = sb("hold", [P, 2], F32)
        expert_no = sb("expert_no", [P, NE], F32)
        token_no = sb("token_no", [P, NT], I32)
        slot_ids = sb("slot_ids", [P, NE * CPE * CT], I32)
        rw = sb("rw", [P, DK * NE], F32)
        rw_hi = sb("rw_hi", [P, DK * NE], F16)
        rw_lo = sb("rw_lo", [P, DK * NE], F16)
        rb_row = sb("rb_row", [P, NE], F32)
        lnw_row = sb("lnw_row", [P, D], F32)
        logits = sb("logits", [P, NE], F32)
        top = sb("top", [P, 8], F32)
        top_i = sb("top_i", [P, 8], U32)
        top_f = sb("top_f", [P, 2], F32)
        oh = sb("oh", [P, 2 * NE], F32)
        oh_all = sb("oh_all", [P, NT * 2 * NE], F32)
        mask = sb("mask", [P, NE], F16)
        gap = sb("gap", [P, NT], F32)
        carry = sb("carry", [P, NE], F32)
        slot_of = sb("slot_of", [P, NE], F32)
        slot_pick = sb("slot_pick", [P, 2 * NE], F32)
        slot_f = sb("slot_f", [P, 2], F32)
        slots = sb("slots", [P, NT * 2], I32)
        cnt = sb("cnt", [1, NE], F32)
        scan = sb("scan", [1, 4, 2 * NE], F32)
        first_slot = sb("first_slot", [P, NE], F32)
        ranges2_f = sb("ranges2_f", [1, 4, NE], F32)
        ranges2 = sb("ranges2", [1, 4, NE], I32)
        chunk_i = sb("chunk_i", [1, MAXC], F32)
        chunk_skip = sb("chunk_skip", [1, MAXC, NE], F32)
        chunk_f = sb("chunk_f", [1, MAXC], F32)
        chunk_at = sb("chunk_at", [1, MAXC], I32)
        gap_e = sb("gap_e", [P, NT], F32)
        wt = sb("wt", [P, 2 * NT], F32)
        cw = sb("cw", [P, NT * NE], F32)
        cw2 = sb("cw2", [P, NT * NE], F32)
        b1t = sb("b1t", [P, NE * FK], F32)
        ids = sb("ids", [P, CT], I32)
        ids_out = sb("ids_out", [P, CT], I32)
        cw_chunk = sb("cw_chunk", [P, CT * NE], F32)
        gx = [counts[:, i * XW:(i + 1) * XW] for i in range(CT)]
        at = CT * XW
        x4 = counts[:, at:at + DK * CH].bitcast(F16)
        at += DK * CH
        y32 = counts[:, at:at + FK * CH]
        at += FK * CH
        y_hi = counts[:, at:at + FK * CH // 2].bitcast(F16)
        at += FK * CH // 2
        y_lo = counts[:, at:at + FK * CH // 2].bitcast(F16)
        assert at + FK * CH // 2 <= NT * NP * 3 // 4
        y_out = [work[:, i * D:(i + 1) * D] for i in range(CT)]
        b2_row = [wbuf1[:, 2 * PIECES * D + i * 2 * D:2 * PIECES * D + (i + 1) * 2 * D].bitcast(F32) for i in range(2)]
        fin = [(wbuf0 if r < PIECES else wbuf1)[:, r % PIECES * 2 * D:(r % PIECES + 1) * 2 * D].bitcast(F32)
               for r in range(NT)]
        stats5 = oh_all[:, 0:NT * 12].rearrange("p (r s) -> p r s", s=12)
        mv5 = cw2[:, 0:2 * NT].rearrange("p (r s) -> p r s", s=2)
        var5, std5, rstd5, q5, shift5 = [cw2[:, (2 + i) * NT:(3 + i) * NT] for i in range(5)]
        e_hi = [w[:, 0:PIECES * D] for w in (wbuf0, wbuf1)]
        e_lo = [w[:, PIECES * D:2 * PIECES * D] for w in (wbuf0, wbuf1)]

        onehots = wbuf1[0:EP, 0:GROUP * OHW]
        zero_row = wbuf1[:, GROUP * OHW:GROUP * OHW + 2 * D].bitcast(F32)
        XT_AT = 2 * (NT - 2) * D
        assert GROUP * OHW + 2 * D <= XT_AT
        xt = wbuf1[:, XT_AT:]
        w_hi, w_lo = e_hi[0], e_lo[0]
        hs = wbuf1[:]

        ps = ctx.enter_context(nc.psum_tensor("ps", [P, 8 * HALF], F32))

        def bank(i, n=1):
            return ps[:, i * HALF:(i + n) * HALF]

        count_ps = ps[:, 0:NP]
        xt_ps = bank(3, 2)
        lin_ps = bank(5, 2)
        misc_ps = bank(7)
        deg_lo_ps = misc_ps[:, 48:48 + NT]
        agg_ps = [bank(0, 2), bank(2, 2)]
        x2t_ps = bank(4, 2)
        router_ps = bank(6)
        rank_ps = bank(7)
        up_ps = [ps[:, c * HALF:c * HALF + CH] for c in range(FK)]
        x4_ps = [ps[:, (4 + i) * HALF:(4 + i) * HALF + CH] for i in range(2)]
        down_ps = [bank(6), bank(7)]

        agg_done = sem("agg_done")
        b_in = sem("b_in")
        blank = sem("blank")
        chunks_done = sem("chunks_done")
        consts_done = sem("consts_done")
        consts_in = sem("consts_in")
        count_done = sem("count_done")
        count_hi_read = sem("count_hi_read")
        count_lo_8 = sem("count_lo_8")
        count_lo_done = sem("count_lo_done")
        count_lo_read = sem("count_lo_read")
        cw_copied = sem("cw_copied")
        cw_done = sem("cw_done")
        cw_stored = sem("cw_stored")
        deg_done = sem("deg_done")
        deg_hi_done = sem("deg_hi_done")
        deg_sqrt = sem("deg_sqrt")
        deg_summed = sem("deg_summed")
        dis_done = sem("dis_done")
        down_done = sem("down_done")
        down_read = sem("down_read")
        dst_rows_in = sem("dst_rows_in")
        dve_step = sem("dve_step")
        dve_step3 = sem("dve_step3")
        dve_step4 = sem("dve_step4")
        dve_step5 = sem("dve_step5")
        e_lo_done = sem("e_lo_done")
        edges_in = sem("edges_in")
        fin_added = sem("fin_added")
        fin_added_dve = sem("fin_added_dve")
        fin_weighted = sem("fin_weighted")
        gap_done = sem("gap_done")
        gap_exp = sem("gap_exp")
        gelu_done = sem("gelu_done")
        hs_hi_done = sem("hs_hi_done")
        hs_lo_done = sem("hs_lo_done")
        ids_in = sem("ids_in")
        lin_done = sem("lin_done")
        lin_read = sem("lin_read")
        lnb_in = sem("lnb_in")
        mask_done = sem("mask_done")
        onehot_done = sem("onehot_done")
        onehot_used = sem("onehot_used")
        out_stored = sem("out_stored")
        over_cols = sem("over_cols")
        over_done = sem("over_done")
        over_ps = sem("over_ps")
        pool_step4 = sem("pool_step4")
        ranges2_done = sem("ranges2_done")
        ranges_done = sem("ranges_done")
        rank_done = sem("rank_done")
        router_done = sem("router_done")
        rows_added = sem("rows_added")
        rstd5_done = sem("rstd5_done")
        rw_hi_done = sem("rw_hi_done")
        rw_lo_done = sem("rw_lo_done")
        scaled = sem("scaled")
        scattered = sem("scattered")
        slots_done = sem("slots_done")
        spans_cols = sem("spans_cols")
        spans_n = sem("spans_n")
        spans_ps = sem("spans_ps")
        spans_tr = sem("spans_tr")
        spare_in = sem("spare_in")
        std5_done = sem("std5_done")
        std_done = sem("std_done")
        table_in = sem("table_in")
        table_loaded = sem("table_loaded")
        up_done = sem("up_done")
        var5_done = sem("var5_done")
        var_done = sem("var_done")
        w_hi_done = sem("w_hi_done")
        w_lo_done = sem("w_lo_done")
        w_scaled = sem("w_scaled")
        x0_in = sem("x0_in")
        x1_in = sem("x1_in")
        x1b_done = sem("x1b_done")
        x2_stored = sem("x2_stored")
        x2t_done = sem("x2t_done")
        x2t_hi_done = sem("x2t_hi_done")
        x2t_lo_done = sem("x2t_lo_done")
        x4_done = sem("x4_done")
        x4_hi_done = sem("x4_hi_done")
        x4_lo_done = sem("x4_lo_done")
        x_again0 = sem("x_again0")
        x_again1 = sem("x_again1")
        xn_done = sem("xn_done")
        xrest_in = sem("xrest_in")
        xs_done = sem("xs_done")
        xs_hi_done = sem("xs_hi_done")
        xt_done = sem("xt_done")
        xt_hi_done = sem("xt_hi_done")
        xt_lo_done = sem("xt_lo_done")
        y_lo_done = sem("y_lo_done")
        y_ready = sem("y_ready")
        y_ready_b2 = sem("y_ready_b2")
        carrier = sem("carrier")
        gathered = [sem(f"gathered{i}") for i in range(CT)]
        added = [sem(f"added{i}") for i in range(CT)]
        fin_in = [sem(f"fin_in{i}") for i in range(NT)]
        stage_in = [sem(f"stage_in{i}") for i in range(STAGES)]
        b2_in = [sem(f"b2_in{i}") for i in range(2)]

        def settle(eng):
            eng.sem_inc(carrier, 1)

        block = ctx.enter_context(nc.Block())

        @block.gpsimd
        def _(pool):
            g = nc.gpsimd
            for c in (g.iota(block_lo[:], [[P, NT]], base=0, channel_multiplier=0, allow_small_or_imprecise_dtypes=True),
                      g.iota(block_hi[:], [[P, NT]], base=P, channel_multiplier=0, allow_small_or_imprecise_dtypes=True),
                      g.iota(tile_no[:], [[P, 2]], base=0, channel_multiplier=1, allow_small_or_imprecise_dtypes=True),
                      g.iota(step_from[:], [[GROUP, NSTEP]], base=0, channel_multiplier=0,
                             allow_small_or_imprecise_dtypes=True),
                      g.memset(span[:], 0.0)):
                c.then_inc(consts_done, 1)
            pool.wait_ge(blank, 2)
            g.affine_select(out=ident[:], in_=ident[:], compare_op=ALU.not_equal, fill=1.0, base=0,
                            pattern=[[-1, P]], channel_multiplier=1).then_inc(consts_done, 1)
            g.affine_select(out=tri[:], in_=tri[:], compare_op=ALU.is_gt, fill=0.0, base=0,
                            pattern=[[1, NT]], channel_multiplier=-1).then_inc(consts_done, 1)
            g.iota(iota16[:], [[1, NP]], base=0, channel_multiplier=0,
                   allow_small_or_imprecise_dtypes=True).then_inc(consts_done, 1)
            pool.wait_ge(blank, 5)
            g.affine_select(out=ident16[:], in_=ident16[:], compare_op=ALU.not_equal, fill=1.0, base=0,
                            pattern=[[-1, P]], channel_multiplier=1).then_inc(consts_done, 1)
            g.affine_select(out=eye_wide[:], in_=eye_wide[:], compare_op=ALU.not_equal, fill=1.0, base=NP - P,
                            pattern=[[-1, 2 * NP - P]], channel_multiplier=1).then_inc(consts_done, 1)
            g.affine_select(out=tri16[:], in_=tri16[:], compare_op=ALU.is_gt, fill=0.0, base=0,
                            pattern=[[1, P]], channel_multiplier=-1).then_inc(consts_done, 1)
            for c in (g.memset(ones16[:], 1.0),
                      g.iota(expert_no[:], [[1, NE]], base=0, channel_multiplier=0, allow_small_or_imprecise_dtypes=True),
                      g.iota(first_slot[:], [[CAP, NE]], base=0, channel_multiplier=0,
                             allow_small_or_imprecise_dtypes=True),
                      g.iota(chunk_i[:], [[1, MAXC]], base=0, channel_multiplier=0, allow_small_or_imprecise_dtypes=True),
                      g.iota(token_no[:], [[P, NT]], base=0, channel_multiplier=1)):
                c.then_inc(consts_done, 1)
            g.iota(slot_ids[:], [[0, NE * CPE], [1, CT]], base=NP, channel_multiplier=CT).then_inc(table_in, 1)
            g.memset(zero_row, 0.0).then_inc(spare_in, 1)

            def split_lo(q, hi, lo):
                s = q % STAGES
                cs = slice(q % PIECES * D, (q % PIECES + 1) * D)
                pool.wait_ge(w_hi_done, q + 1)
                g.tensor_tensor(lo[:, cs], stage[:, s * D:(s + 1) * D], hi[:, cs], ALU.subtract).then_inc(w_lo_done, 1)

            def xs_lo(m):
                pool.wait_ge(xs_hi_done, m + 1)
                g.tensor_tensor(xs[:, D:], xn, xs[:, 0:D], ALU.subtract).then_inc(xs_done, 1)

            def count_lo_8_copy(m):
                pool.wait_ge(count_lo_read, m + 1)
                settle(pool)
                g.tensor_copy(ct_lo_8[:], ct_lo_16[:], saturate=False).then_inc(count_lo_8, 1)
                pool.wait_ge(count_lo_8, m + 1)
                settle(pool)
                g.tensor_copy(ct_lo[:, ds(m * NP, NP)].bitcast(U32), ct_lo_8[:].bitcast(U32)).then_inc(count_lo_done, 1)

            for q in range(PIECES):
                split_lo(q, w_hi, w_lo)
                if q == 1:
                    xs_lo(0)
            xs_lo(1)
            count_lo_8_copy(0)
            with pool.Fori(1, NT - 1) as m:
                xs_lo(m + 1)
                count_lo_8_copy(m)
            count_lo_8_copy(NT - 1)

            def add_lnb(r):
                rs = slice(r * D, (r + 1) * D)
                pool.wait_ge(xn_done, NT + r + 1)
                g.tensor_tensor(t[:, rs], t[:, rs], b_row[:], ALU.add).then_inc(x1b_done, 1)

            pool.wait_ge(lnb_in, 16)
            pool.wait_ge(consts_in, 16 * 5)
            for r in range(NT + 2):
                if r < NT - 1:
                    xs_lo(NT + r)
                if 2 <= r:
                    pool.wait_ge(slots_done, r - 1)
                    for n in range(2):
                        c = 2 * (r - 2) + n
                        g.indirect_dma_start(out=slot_table, out_offset=bass.IndirectOffsetOnAxis(
                            ap=slots[:, c:c + 1].bitcast(U32), axis=0), in_=token_no[:, r - 2:r - 1],
                            in_offset=None).then_inc(scattered, 16)
                if 2 <= r < NT:
                    split_lo(PIECES + r - 2, e_hi[0], e_lo[0])
                if 1 <= r < NT - 1:
                    add_lnb(r - 1)

            st4 = Steps(pool, pool_step4)
            pool.wait_ge(cw_stored, 16)
            pool.wait_ge(x2_stored, 2 * 16 * NT)

            def gather(rows):
                for i in range(CT):
                    g.indirect_dma_start(out=rows[i], out_offset=None, in_=x2_rows,
                                         in_offset=bass.IndirectOffsetOnAxis(ap=ids[:, i:i + 1].bitcast(U32), axis=0)
                                         ).then_inc(gathered[i], 16)

            def chunk_ids(c, into):
                no = pool.value_load(chunk_at[0:1, ds(c, 1)], min_val=0, max_val=NE * CPE - 1)
                st4.did(g.tensor_copy(into[:], slot_ids[:, ds(no * CT, CT)]))
                st4.wait()

            pool.wait_ge(agg_done, 2 * NT)
            pool.wait_ge(ids_in, 16)
            gather(gx0)
            pool.wait_ge(table_loaded, 16)
            pool.wait_ge(chunks_done, 1)
            total = pool.value_load(ranges2[0:1, 1, NE - 1:NE], min_val=1, max_val=MAXC - 2)

            def chunk(c, first):
                st4.enter(2 * c)
                for i in range(CT):
                    pool.wait_ge(gathered[i], 16 * c + 16)
                settle(pool)
                chunk_ids(c + 1, ids)
                if not first:
                    pool.wait_ge(x4_done, DK * c + DK)
                    pool.wait_ge(cw_copied, c + 1)
                    settle(pool)
                gather(gx)
                if first:
                    add_lnb(NT - 2)
                    add_lnb(NT - 1)
                else:
                    for i in range(CT):
                        pool.wait_ge(added[i], 16 * c)
                    pool.sem_inc(rows_added, 1)
                chunk_ids(c, ids_out)
                for i in range(CT):
                    pool.wait_ge(y_ready, CT * c + (i + 1))
                    settle(pool)
                    g.indirect_dma_start(out=acc_rows, out_offset=bass.IndirectOffsetOnAxis(
                        ap=ids_out[:, i:i + 1].bitcast(U32), axis=0), in_=y_out[i], in_offset=None,
                        compute_op=ALU.add).then_inc(added[i], 16)

            chunk(0, True)
            with pool.Fori(1, total) as c:
                chunk(c, False)

            pool.wait_ge(x1b_done, NT)
            for r in range(POOL_TILES):
                rs = slice(r * D, (r + 1) * D)
                pool.wait_ge(scaled, r + 1)
                g.tensor_tensor(fin[r], fin[r], lnw_row[:], ALU.mult).then_inc(fin_weighted, 1)
                pool.wait_ge(fin_weighted, r + 1)
                g.tensor_tensor(t[:, rs], t[:, rs], fin[r], ALU.add).then_inc(fin_added, 1)

        @block.sync
        def _(sp):
            def piece(q, splits):
                if splits:
                    sp.wait_ge(w_lo_done, q - STAGES + 1)
                s = q % STAGES
                sp.dma_start(stage[:, s * D:(s + 1) * D], wst[q // PIECES, q % PIECES]).then_inc(stage_in[s], 16)

            sp.dma_start(dst_r[:, 0, :], dst_rows[0:P, :]).then_inc(dst_rows_in, 16)
            sp.dma_start(dst_r[0:ET - P, 1, :], dst_rows[P:ET, :]).then_inc(dst_rows_in, 16)
            sp.dma_start(t[:, 0:D], x[0:P, :]).then_inc(x0_in, 16)
            sp.dma_start(src_i[:], src).then_inc(edges_in, 16)
            sp.dma_start(dst_i[:], dst).then_inc(edges_in, 16)
            for q in range(STAGES):
                piece(q, False)
            sp.dma_start(t[:, D:2 * D], x[P:2 * P, :]).then_inc(x1_in, 16)
            for q in range(STAGES, PIECES):
                piece(q, True)
            sp.dma_start(b_row[:], b.partition_broadcast(P)).then_inc(b_in, 16)
            sp.dma_start(t[:, 2 * D:].rearrange("p (r d) -> p r d", d=D),
                         x[2 * P:, :].rearrange("(r p) d -> p r d", p=P)).then_inc(xrest_in, 16)
            for q in range(PIECES, PIECES + STAGES):
                piece(q, True)
            for dst_ap, src_ap in ((rw[:], router_w), (rb_row[:], router_b.partition_broadcast(P)), (b1t[:], b1),
                                   (lnw_row[:], ln_w.partition_broadcast(P))):
                sp.dma_start(dst_ap, src_ap).then_inc(consts_in, 16)
            sp.wait_ge(table_in, 1)
            slot_table_v = slot_table.rearrange("(n p t) o -> p n (t o)", p=P, t=CT)
            slot_ids_v = slot_ids[:].rearrange("p (n t) -> p n t", t=CT)
            sp.dma_start(slot_table_v, slot_ids_v).then_inc(consts_in, 16)
            sp.wait_ge(spare_in, 1)
            for i in range(CT):
                rows = slice(NP + i * P, NP + (i + 1) * P)
                sp.dma_start(x2_rows[rows, 0:D], zero_row).then_inc(spare_in, 16)
                sp.dma_start(x2_rows[rows, D:], zero_row[:, 0:NE]).then_inc(spare_in, 16)
                sp.dma_start(acc_rows[rows, :], zero_row).then_inc(spare_in, 16)
            sp.wait_ge(hs_lo_done, 2)
            sp.dma_start(t[:, 0:2 * D].rearrange("p (r d) -> p r d", d=D),
                         x[0:2 * P, :].rearrange("(r p) d -> p r d", p=P)).then_inc(x_again0, 16)
            sp.wait_ge(lin_read, NT)
            sp.dma_start(b_row[:], ln_b.partition_broadcast(P)).then_inc(lnb_in, 16)
            sp.wait_ge(hs_lo_done, NT)
            sp.dma_start(t[:, 2 * D:].rearrange("p (r d) -> p r d", d=D),
                         x[2 * P:, :].rearrange("(r p) d -> p r d", p=P)).then_inc(x_again1, 16)
            for r in range(NT):
                rows = slice(r * P, (r + 1) * P)
                sp.wait_ge(xn_done, NT + r + 1)
                sp.dma_start(acc_rows[rows, :], xn).then_inc(x2_stored, 16)
                sp.wait_ge(xs_done, NT + r + 1)
                sp.dma_start(x2_rows[rows, 0:D], xs.bitcast(F32)).then_inc(x2_stored, 16)
                if 2 <= r:
                    piece(PIECES + STAGES + r - 2, True)
            sp.wait_ge(cw_done, 1)
            sp.dma_start(x2_rows[0:NP, D:].rearrange("(r p) e -> p r e", p=P),
                         cw[:].rearrange("p (r e) -> p r e", e=NE)).then_inc(cw_stored, 16)
            sp.wait_ge(scattered, 16 * 2 * NT)
            sp.dma_start(ids[:], slot_table_v[:, 0, :]).then_inc(ids_in, 16)
            sp.dma_start(slot_ids_v, slot_table_v).then_inc(table_loaded, 16)
            pieces = wst.rearrange("i q p d -> (i q) p d")
            with sp.Fori(PIECES // STAGES * 2 + 1, (NE + 1) * PIECES // STAGES) as u:
                for s in range(STAGES):
                    sp.wait_ge(e_lo_done, u * STAGES + (s - STAGES + 1 - 2 * PIECES))
                    sp.dma_start(stage[:, s * D:(s + 1) * D], pieces[ds(u * STAGES + s, 1)].rearrange("o p d -> (o p) d")
                                 ).then_inc(stage_in[s], 16)
            total = sp.value_load(ranges2[0:1, 1, NE - 1:NE], min_val=1, max_val=MAXC - 2)
            for i in range(CT):
                sp.wait_ge(added[i], total * 16)
            settle(sp)
            for r in range(NT):
                sp.dma_start(fin[r], acc_rows[r * P:(r + 1) * P, :]).then_inc(fin_in[r], 16)
            for r in range(POOL_TILES):
                sp.wait_ge(fin_added, r + 1)
                sp.dma_start(out[r * P:(r + 1) * P, :], t[:, r * D:(r + 1) * D]).then_inc(out_stored, 16)
            sp.wait_ge(out_stored, 16 * NT)

        @block.scalar
        def _(act):
            a = nc.scalar

            scaled_of = Steps(act, w_scaled)

            def split_hi(q, hi):
                s, j = q % STAGES, q % PIECES
                piece = stage[:, s * D:(s + 1) * D]
                act.wait_ge(stage_in[s], (q // STAGES) * 16 + 16)
                scaled_of.link(a.activation(piece, piece, ACT.Copy, scale=WSCALE))
                a.activation(hi[:, j * D:(j + 1) * D], piece, ACT.Copy).then_inc(w_hi_done, 1)

            def sqrt_var(n):
                act.wait_ge(var_done, n)
                a.activation(std[:, 1:2], std[:, 0:1], ACT.Sqrt).then_inc(std_done, 1)

            def xs_hi(m):
                act.wait_ge(xn_done, m + 1)
                act.wait_ge(xt_done, m)
                a.activation(xs[:, 0:D], xn, ACT.Copy).then_inc(xs_hi_done, 1)

            def count_hi(m):
                act.wait_ge(count_done, m + 1)
                settle(act)
                a.activation(ct_hi[:, ds(m * NP, NP)], count_ps, ACT.Copy).then_inc(count_hi_read, 1)

            def xt_hi(m):
                act.wait_ge(xt_done, m + 1)
                settle(act)
                a.activation(xt[:, ds((m % 2) * 2 * D, D)], xt_ps, ACT.Copy).then_inc(xt_hi_done, 1)

            for q in range(PIECES):
                split_hi(q, w_hi)
                if q == 0:
                    sqrt_var(1)
                if q == 1:
                    act.wait_ge(xn_done, 1)
                    a.activation(xs[:, 0:D], xn, ACT.Copy).then_inc(xs_hi_done, 1)
                if q == 4:
                    xt_hi(0)
            sqrt_var(2)
            count_hi(0)
            xs_hi(1)
            with act.Fori(1, NT - 1) as m:
                count_hi(m)
                sqrt_var(m + 2)
                xt_hi(m)
                xs_hi(m + 1)
            count_hi(NT - 1)
            xt_hi(NT - 1)

            act.wait_ge(deg_summed, 1)
            a.activation(deg_s[:], deg_f[:], ACT.Sqrt).then_inc(deg_sqrt, 1)
            act.wait_ge(spare_in, 1 + 16 * 3 * CT)
            act.wait_ge(count_done, NT)
            act.wait_ge(dis_done, 1)

            def hs_hi(m):
                a.activation(hs[:, ds(m * 2 * D, D)], t[:, ds(m * D, D)], ACT.Copy,
                             scale=dis[:, ds(m, 1)]).then_inc(hs_hi_done, 1)

            act.wait_ge(lin_read, NT - 1)
            with act.Fori(0, NT - 1) as m:
                hs_hi(m)
            act.wait_ge(lin_read, NT)
            hs_hi(NT - 1)

            act.wait_ge(consts_in, 16 * 5)
            a.activation(rw_hi[:], rw[:], ACT.Copy, scale=WSCALE).then_inc(rw_hi_done, 1)
            for r in range(NT + 1):
                if r >= 1:
                    act.wait_ge(x2t_done, r)
                    act.wait_ge(router_done, r - 1)
                    a.activation(x2t[:, 0:D], x2t_ps, ACT.Copy).then_inc(x2t_hi_done, 1)
                if r < NT:
                    sqrt_var(NT + r + 1)
                    act.wait_ge(xn_done, NT + r + 1)
                    act.wait_ge(x2t_done, r)
                    act.wait_ge(x2_stored, 2 * 16 * r)
                    a.activation(xs[:, 0:D], xn, ACT.Copy).then_inc(xs_hi_done, 1)
                if 2 <= r < NT:
                    split_hi(PIECES + r - 2, e_hi[0])
            act.wait_ge(gap_done, 1)
            a.activation(gap_e[:], gap[:], ACT.Exp).then_inc(gap_exp, 1)

            act.wait_ge(agg_done, 2 * NT)
            act.dma_start(b2_row[0], b2[0:1, :].rearrange("o d -> (o d)").partition_broadcast(P)).then_inc(b2_in[0], 16)
            act.sem_inc(gelu_done, FK)

            def turned(c, j):
                act.wait_ge(x4_done, c * DK + (j + 1))
                a.activation(x4[:, j * 2 * CH:(2 * j + 1) * CH], x4_ps[j % 2], ACT.Copy).then_inc(x4_hi_done, 1)

            def piece_hi(e, j, split):
                s = j % STAGES
                act.wait_ge(stage_in[s], (e + 2) * (16 * PIECES // STAGES) + 16 * (j // STAGES + 1))
                a.activation(split[:, j * D:(j + 1) * D], stage[:, s * D:(s + 1) * D], ACT.Copy,
                             scale=WSCALE).then_inc(w_hi_done, 1)

            for j in range(EARLY):
                piece_hi(0, j, e_hi[1])
            for j in range(DK):
                turned(0, j)
            act.wait_ge(ranges2_done, 1)

            def chunk(c, e, split, first=False):
                if split is not None and not first:
                    for j in range(EARLY):
                        piece_hi(e, j, split)
                for f in range(FK):
                    act.wait_ge(up_done, c * FK + (f + 1))
                    settle(act)
                    a.activation(y32[:, f * CH:(f + 1) * CH], up_ps[f], ACT.Gelu, bias=b1t[:, ds(e * FK + f, 1)],
                                 scale=1.0 / WSCALE).then_inc(gelu_done, 1)
                for j in range(DK):
                    turned(c + 1, j)
                    if split is not None and 2 <= j < 2 + PIECES - EARLY:
                        piece_hi(e, EARLY + j - 2, split)

            def expert(e, h, split, first=False):
                c0 = act.value_load(ranges2[0:1, 0, ds(e, 1)], min_val=0, max_val=MAXC - 3)
                c1 = act.value_load(ranges2[0:1, 1, ds(e, 1)], min_val=1, max_val=MAXC - 2)
                more = act.value_load(ranges2[0:1, 3, ds(e, 1)], min_val=0, max_val=1)
                act.wait_ge(down_done, c0 * (2 * CT) + 1)
                if split is not None:
                    act.wait_ge(y_ready_b2, c0 + 1)
                    act.dma_start(b2_row[1 - h], b2[ds(e + 1, 1), :].rearrange("o d -> (o d)").partition_broadcast(P)
                                  ).then_inc(b2_in[1 - h], 16)
                chunk(0 if first else c0, e, split, first)
                with act.If(more):
                    with act.Fori(c0 + 1, c1) as c:
                        chunk(c, e, None)

            expert(0, 0, e_hi[1], True)
            expert(1, 1, e_hi[0])
            with act.Fori(1, NE // 2 - 1) as pair:
                for h in range(2):
                    expert(pair * 2 + h, h, e_hi[1 - h])
            expert(NE - 2, 0, e_hi[1])
            expert(NE - 1, 1, None)

            for n, tiles in enumerate(LAST_GROUPS):
                cs = slice(tiles[0], tiles[-1] + 1)
                act.wait_ge(var5_done, n + 1)
                a.activation(std5[:, cs], var5[:, cs], ACT.Sqrt).then_inc(std5_done, 1)
                act.wait_ge(rstd5_done, n + 1)
                for r in tiles:
                    if r < POOL_TILES:
                        ins = a.activation(fin[r], fin[r], ACT.Identity, bias=shift5[:, r:r + 1], scale=rstd5[:, r:r + 1])
                    else:
                        ins = a.activation(fin[r], fin[r], ACT.Copy, scale=rstd5[:, r:r + 1])
                    ins.then_inc(scaled, 1)
            for r in range(POOL_TILES, NT):
                act.wait_ge(fin_added_dve, r - POOL_TILES + 1)
                act.dma_start(out[r * P:(r + 1) * P, :], t[:, r * D:(r + 1) * D]).then_inc(out_stored, 16)
            act.wait_ge(out_stored, 16 * NT)

        @block.vector
        def _(dve):
            v = nc.vector
            step = Steps(dve, dve_step)

            def newton(r, x, q, steps):
                steps.link(v.tensor_tensor(q, r, x, ALU.mult))
                steps.link(v.tensor_tensor(q, q, r, ALU.mult))
                steps.link(v.tensor_scalar(q, q, -0.5, 1.5, ALU.mult, ALU.add))
                return v.tensor_tensor(r, r, q, ALU.mult)

            def carry_wait(col):
                v.tensor_copy(hold[:, 0:1], col)

            def layernorm_stats(xm, eps, steps):
                steps.did(v.bn_stats(stats[:, 0:6], xm[0]))
                steps.did(v.bn_stats(stats[:, 6:12], xm[1]))
                steps.wait()
                carry_wait(stats[:, 0:1])
                steps.link(v.bn_aggr(mv[:], stats[:]))
                return v.tensor_scalar(std[:, 0:1], mv[:, 1:2], eps, None, ALU.add)

            def layernorm_a(m):
                xm = t[:, ds(m * D, HALF)], t[:, ds(m * D + HALF, HALF)]
                layernorm_stats(xm, EPS1, step).then_inc(var_done, 1)

            def layernorm_b(m):
                dve.wait_ge(std_done, m + 1)
                step.link(v.reciprocal(rstd[:], std[:, 1:2]))
                step.link(newton(rstd[:], std[:, 0:1], q_col[:], step))
                dve.wait_ge(xs_done, m)
                v.tensor_scalar(xn, t[:, ds(m * D, D)], mv[:, 0:1], rstd[:],
                                ALU.subtract, ALU.mult).then_inc(xn_done, 1)

            v.memset(ident[:], 0.0).then_inc(blank, 1)
            v.memset(tri[:], 1.0).then_inc(blank, 1)
            v.memset(ident16[:], 0.0).then_inc(blank, 1)
            v.memset(eye_wide[:], 0.0).then_inc(blank, 1)
            v.memset(tri16[:], 1.0).then_inc(blank, 1)
            step.did(v.memset(first_v[:], 0.0))
            step.did(v.memset(last_v[:], 0.0))
            dve.wait_ge(dst_rows_in, 32)
            dve.wait_ge(consts_done, RANGE_CONSTS)
            step.did(v.tensor_scalar(tile_from[:], tile_no[:], -1.0, BIG, ALU.mult, ALU.add))
            step.did(v.tensor_scalar(tile_to[:], tile_no[:], 1.0, None, ALU.add))
            halves = ((0, P), (1, ET - P))
            for h, n in halves:
                step.did(v.tensor_copy(dst_rf[0:n, h, :], dst_r[0:n, h, :]))
            step.wait()
            for h, n in halves:
                step.did(v.tensor_reduce(tile_min[0:n, h:h + 1], dst_rf[0:n, h, :], AXX, ALU.min))
                step.did(v.tensor_reduce(tile_max[0:n, h:h + 1], dst_rf[0:n, h, :], AXX, ALU.max))
            step.wait()
            for h, n in halves:
                step.did(v.tensor_scalar(overlap[0:n, h, 0:NT], block_lo[0:n, :], tile_max[0:n, h:h + 1], None, ALU.is_le))
            step.wait()
            for h, n in halves:
                ov = overlap[0:n, h, 0:NT]
                step.did(v.scalar_tensor_tensor(ov, block_hi[0:n, :], tile_min[0:n, h:h + 1], ov, ALU.is_gt, ALU.mult))
            step.wait()
            for h, n in halves:
                ov = overlap[0:n, h, 0:NT]
                step.did(v.tensor_scalar(first_v[0:n, h, 0:NT], ov, tile_from[0:n, h:h + 1], None, ALU.mult))
                step.did(v.tensor_scalar(last_v[0:n, h, 0:NT], ov, tile_to[0:n, h:h + 1], None, ALU.mult))
            step.wait()
            v.engine_nop().then_inc(spans_cols, 1)
            dve.wait_ge(x0_in, 16)
            layernorm_a(0)
            dve.wait_ge(spans_tr, 1)
            step.did(v.tensor_reduce(span[0:NT, 0:1], misc_ps[0:NT, 0:2 * P], AXX, ALU.max))
            step.link(v.tensor_reduce(span[0:NT, 1:2], misc_ps[0:NT, 2 * P:4 * P], AXX, ALU.max))
            step.link(v.tensor_scalar(span[0:NT, 2:3], span[0:NT, 0:1], -1.0, BIG, ALU.mult, ALU.add))
            step.did(v.tensor_scalar(span[0:NT, 3:4], span[0:NT, 2:3], ET - 1.0, None, ALU.min))
            step.link(v.tensor_tensor(span[0:NT, 4:5], span[0:NT, 1:2], span[0:NT, 2:3], ALU.subtract))
            step.link(v.tensor_scalar(span[0:NT, 4:5], span[0:NT, 4:5], 1.0, None, ALU.max))
            step.link(v.tensor_scalar(steps_in[0:NT, :], step_from[0:NT, :], span[0:NT, 4:5], None, ALU.is_lt))
            v.tensor_reduce(span[0:NT, 5:6], steps_in[0:NT, :], AXX, ALU.add).then_inc(spans_n, 1)
            dve.wait_ge(edges_in, 32)
            step.did(v.memset(src_f[:, ET:], -1.0))
            step.did(v.memset(dst_f[:, ET:], -1.0))
            step.did(v.tensor_copy(src_f[:, 0:ET], src_i[:]))
            step.did(v.tensor_copy(dst_f[:, 0:ET], dst_i[:]))
            layernorm_b(0)
            dve.wait_ge(spans_ps, 1)
            step.link(v.tensor_copy(span_row[0:1, 0:48], misc_ps[0:1, 0:48]))
            step.did(v.tensor_copy(ranges[0:1, 0, 0:NT], span_row[0:1, 0:NT]))
            step.did(v.tensor_tensor(ranges[0:1, 1, 0:NT], span_row[0:1, 0:NT], span_row[0:1, 16:16 + NT], ALU.add))
            v.scalar_tensor_tensor(ranges[0:1, 2, 0:NT], span_row[0:1, 0:NT], -float(GROUP),
                                   span_row[0:1, 32:32 + NT], ALU.mult, ALU.add).then_inc(ranges_done, 1)
            dve.wait_ge(ranges_done, 1)
            step.wait()

            def edge_onehots(m):
                i0 = dve.value_load(ranges[0:1, 0, ds(m, 1)], min_val=0, max_val=NT * NSTEP)
                i1 = dve.value_load(ranges[0:1, 1, ds(m, 1)], min_val=1, max_val=NT * NSTEP)
                off = dve.value_load(ranges[0:1, 2, ds(m, 1)], min_val=-NT * ETP, max_val=ET)
                with dve.Fori(i0, i1) as i:
                    k = dve.snap(i * GROUP + off).with_bounds(min_val=0, max_val=ETP - GROUP)
                    for u in range(GROUP):
                        if u % SUB == 0:
                            dve.wait_ge(onehot_used, i * (GROUP // SUB) + (u // SUB + 1))
                        v.tensor_scalar(onehots[:, u * OHW:u * OHW + NP], iota16[0:EP, :], src_f[:, ds(k + u, 1)],
                                        None, ALU.is_equal)
                        ins = v.tensor_scalar(onehots[:, u * OHW + NP:(u + 1) * OHW], iota16[0:EP, ds(m * P, P)],
                                              dst_f[:, ds(k + u, 1)], None, ALU.is_equal)
                        if u % SUB == SUB - 1:
                            ins.then_inc(onehot_done, 1)

            def count_lo(m):
                dve.wait_ge(count_hi_read, m + 1)
                dve.wait_ge(count_lo_done, m)
                v.tensor_tensor(ct_lo_16[:], count_ps, ct_hi[:, ds(m * NP, NP)], ALU.subtract).then_inc(count_lo_read, 1)

            def xt_lo(m):
                dve.wait_ge(xt_hi_done, m + 1)
                v.tensor_tensor(xt[:, ds((m % 2) * 2 * D + D, D)], xt_ps, xt[:, ds((m % 2) * 2 * D, D)],
                                ALU.subtract).then_inc(xt_lo_done, 1)

            def h_copy(m):
                dve.wait_ge(lin_done, m + 1)
                for n in range(2):
                    ins = v.scalar_tensor_tensor(t[:, ds(m * D + n * HALF, HALF)], lin_ps[:, n * HALF:(n + 1) * HALF],
                                                 1.0 / WSCALE, b_row[:, n * HALF:(n + 1) * HALF], ALU.mult, ALU.add)
                ins.then_inc(lin_read, 1)

            dve.wait_ge(consts_done, EDGE_CONSTS)
            dve.sem_inc(onehot_used, GROUP // SUB)
            edge_onehots(0)
            dve.wait_ge(x1_in, 16)
            layernorm_a(1)
            xt_lo(0)
            count_lo(0)
            layernorm_b(1)
            edge_onehots(1)
            dve.wait_ge(b_in, 16)
            dve.wait_ge(xrest_in, 16)
            base = step.k
            LINKS1 = 8
            with dve.Fori(1, NT - 1) as m:
                step.enter((m - 1) * LINKS1 + base)
                layernorm_a(m + 1)
                count_lo(m)
                layernorm_b(m + 1)
                xt_lo(m)
                edge_onehots(m + 1)
                h_copy(m - 1)
                assert step.k == LINKS1
            step.enter((NT - 2) * LINKS1 + base)
            count_lo(NT - 1)
            h_copy(NT - 2)
            xt_lo(NT - 1)

            dve.wait_ge(deg_hi_done, 1)
            step.link(v.tensor_copy(deg_f[:], misc_ps[:, 0:NT]))
            v.tensor_scalar(over[:], misc_ps[:, 0:NT], EXACT16, None, ALU.is_ge).then_inc(over_cols, 1)
            dve.wait_ge(over_ps, 1)
            step.link(v.tensor_reduce(over_row[0:1, 0:1], misc_ps[0:1, 16:16 + NT], AXX, ALU.max))
            v.tensor_copy(over_i[0:1, 0:1], over_row[0:1, 0:1]).then_inc(over_done, 1)
            dve.wait_ge(deg_done, 1)
            v.tensor_tensor(deg_f[:], deg_f[:], deg_lo_ps, ALU.add).then_inc(deg_summed, 1)
            dve.wait_ge(deg_sqrt, 1)
            step.link(v.reciprocal(dis[:], deg_s[:]))
            newton(dis[:], deg_f[:], q_dis[:], step).then_inc(dis_done, 1)
            dve.wait_ge(dis_done, 1)

            def hs_lo(m):
                dve.wait_ge(hs_hi_done, m + 1)
                v.scalar_tensor_tensor(hs[:, ds(m * 2 * D + D, D)], t[:, ds(m * D, D)], dis[:, ds(m, 1)],
                                       hs[:, ds(m * 2 * D, D)], ALU.mult, ALU.subtract).then_inc(hs_lo_done, 1)

            with dve.Fori(0, NT - 1) as m:
                hs_lo(m)
            h_copy(NT - 1)
            hs_lo(NT - 1)

            st3 = Steps(dve, dve_step3)
            dve.wait_ge(consts_in, 16 * 5)
            dve.wait_ge(rw_hi_done, 1)
            v.scalar_tensor_tensor(rw_lo[:], rw[:], WSCALE, rw_hi[:], ALU.mult, ALU.subtract).then_inc(rw_lo_done, 1)
            st3.link(v.tensor_copy(carry[:], first_slot[:]))

            def x2t_lo(r):
                dve.wait_ge(x2t_hi_done, r + 1)
                v.tensor_tensor(x2t[:, D:], x2t_ps, x2t[:, 0:D], ALU.subtract).then_inc(x2t_lo_done, 1)

            def add_agg(r):
                dve.wait_ge(x_again0, 16)
                if r >= 2:
                    dve.wait_ge(x_again1, 16)
                for n in range(2):
                    cs = slice(r * D + n * HALF, r * D + (n + 1) * HALF)
                    dve.wait_ge(agg_done, 2 * r + n + 1)
                    st3.did(v.scalar_tensor_tensor(t[:, cs], agg_ps[r % 2][:, n * HALF:(n + 1) * HALF], dis[:, r:r + 1],
                                                   t[:, cs], ALU.mult, ALU.add))
                st3.wait()
                layernorm_stats((t[:, r * D:r * D + HALF], t[:, r * D + HALF:(r + 1) * D]), EPS1, st3
                                ).then_inc(var_done, 1)
                if 1 <= r < NT - 1:
                    x2t_lo(r - 1)
                dve.wait_ge(std_done, NT + r + 1)
                st3.link(v.reciprocal(rstd[:], std[:, 1:2]))
                st3.link(newton(rstd[:], std[:, 0:1], q_col[:], st3))
                dve.wait_ge(xs_done, NT + r)
                dve.wait_ge(x2_stored, 2 * 16 * r)
                v.tensor_scalar(xn, t[:, r * D:(r + 1) * D], mv[:, 0:1], rstd[:], ALU.subtract,
                                ALU.mult).then_inc(xn_done, 1)
                if r == NT - 1:
                    x2t_lo(r - 1)
                    dve.wait_ge(xs_hi_done, NT + r + 1)
                    v.tensor_tensor(xs[:, D:], xn, xs[:, 0:D], ALU.subtract).then_inc(xs_done, 1)

            def choose(r):
                dve.wait_ge(router_done, r + 1)
                st3.link(v.scalar_tensor_tensor(logits[:], router_ps[:, 0:NE], 1.0 / WSCALE, rb_row[:], ALU.mult, ALU.add))
                st3.link(v.max(top[:], logits[:]))
                st3.did(v.tensor_tensor(gap[:, r:r + 1], top[:, 1:2], top[:, 0:1], ALU.subtract))
                st3.link(v.max_index(top_i[:], top[:], logits[:]))
                st3.link(v.tensor_copy(top_f[:], top_i[:, 0:2]))
                for n in range(2):
                    st3.did(v.tensor_scalar(oh[:, n * NE:(n + 1) * NE], expert_no[:], top_f[:, n:n + 1], None,
                                            ALU.is_equal))
                st3.wait()
                v.tensor_tensor(mask[:], oh[:, 0:NE], oh[:, NE:2 * NE], ALU.add).then_inc(mask_done, 1)
                st3.did(v.tensor_copy(oh_all[:, r * 2 * NE:(r + 1) * 2 * NE], oh[:]))

            def place(r):
                dve.wait_ge(rank_done, r + 1)
                st3.link(v.tensor_tensor(slot_of[:], rank_ps[:, 0:NE], carry[:], ALU.add))
                st3.link(v.tensor_tensor(slot_pick[:].rearrange("p (n e) -> p n e", n=2),
                                         oh[:].rearrange("p (n e) -> p n e", n=2),
                                         slot_of[:].unsqueeze(1).to_broadcast([P, 2, NE]), ALU.mult))
                st3.link(v.tensor_reduce(slot_f[:], slot_pick[:].rearrange("p (n e) -> p n e", n=2), AXX, ALU.add))
                v.tensor_copy(slots[:, 2 * r:2 * r + 2], slot_f[:]).then_inc(slots_done, 1)
                if r == NT - 1:
                    st3.link(v.tensor_tensor(cnt[:], rank_ps[0:1, 2 * NE:3 * NE], carry[0:1, :], ALU.add))
                    st3.link(v.tensor_tensor(cnt[:], cnt[:], first_slot[0:1, :], ALU.subtract))
                else:
                    st3.link(v.tensor_tensor(carry[:], rank_ps[:, NE:2 * NE], carry[:], ALU.add))

            for r in range(NT + 2):
                if 2 <= r:
                    choose(r - 2)
                if r < NT:
                    add_agg(r)
                if r == NT:
                    x2t_lo(r - 1)
                if r == NT + 1:
                    st3.wait()
                    v.engine_nop().then_inc(gap_done, 1)
                if 2 <= r:
                    place(r - 2)
            dve.wait_ge(gap_exp, 1)
            st3.link(v.tensor_scalar(wt[:, NT:], gap_e[:], 1.0, None, ALU.add))
            st3.link(v.reciprocal(wt[:, 0:NT], wt[:, NT:]))
            st3.link(v.tensor_tensor(wt[:, NT:], gap_e[:], wt[:, 0:NT], ALU.mult))
            oh_v = oh_all[:].rearrange("p (r n e) -> p n r e", n=2, e=NE)
            for n, d in ((0, cw), (1, cw2)):
                st3.did(v.tensor_tensor(d[:].rearrange("p (r e) -> p r e", e=NE), oh_v[:, n],
                                        wt[:, n * NT:(n + 1) * NT].unsqueeze(2).to_broadcast([P, NT, NE]), ALU.mult))
            st3.wait()
            v.tensor_tensor(cw[:], cw[:], cw2[:], ALU.add).then_inc(cw_done, 1)
            st3.did(v.memset(scan[:], 0.0))
            st3.link(v.tensor_scalar(ranges2_f[:, 0, :], cnt[:], float(CH), 1.0, ALU.is_gt, ALU.add))
            for k in range(2, CPE):
                st3.link(v.scalar_tensor_tensor(ranges2_f[:, 0, :], cnt[:], float(k * CH), ranges2_f[:, 0, :],
                                                ALU.is_gt, ALU.add))
            st3.link(v.tensor_copy(scan[:, 0, NE:], ranges2_f[:, 0, :]))
            for k in range(3):
                st3.link(v.tensor_tensor(scan[:, k + 1, NE:], scan[:, k, NE:], scan[:, k, NE - 2 ** k:2 * NE - 2 ** k],
                                         ALU.add))
            st3.did(v.tensor_copy(ranges2_f[:, 1, :], scan[:, 3, NE:]))
            st3.did(v.tensor_scalar(ranges2_f[:, 3, :], ranges2_f[:, 0, :], 1.0, 1.0, ALU.subtract, ALU.min))
            st3.did(v.tensor_scalar(ranges2_f[:, 2, :], ranges2_f[:, 0, :], -1.0, float(CPE), ALU.mult, ALU.add))
            st3.link(v.tensor_tensor(scan[:, 0, 0:NE], scan[:, 3, NE:], ranges2_f[:, 0, :], ALU.subtract))
            st3.link(v.tensor_copy(ranges2_f[:, 0, :], scan[:, 0, 0:NE]))
            v.tensor_copy(ranges2[:], ranges2_f[:]).then_inc(ranges2_done, 1)
            over_e = [1, MAXC, NE]
            st3.link(v.tensor_tensor(chunk_skip[:], chunk_i[:].unsqueeze(2).to_broadcast(over_e),
                                     ranges2_f[:, 1, :].unsqueeze(1).to_broadcast(over_e), ALU.is_ge))
            st3.link(v.tensor_tensor(chunk_skip[:], chunk_skip[:],
                                     ranges2_f[:, 2, :].unsqueeze(1).to_broadcast(over_e), ALU.mult))
            st3.link(v.tensor_reduce(chunk_f[:], chunk_skip[:], AXX, ALU.add))
            st3.link(v.tensor_tensor(chunk_f[:], chunk_f[:], chunk_i[:], ALU.add))
            v.tensor_scalar(chunk_at[:], chunk_f[:], float(NE * CPE - 1), None, ALU.min).then_inc(chunks_done, 1)

            st4 = Steps(dve, dve_step4)
            dve.sem_inc(x4_lo_done, 2)
            dve.sem_inc(down_read, 2)
            dve.sem_inc(y_ready_b2, 1)
            dve.sem_inc(rows_added, 1)

            def turned(c, j):
                dve.wait_ge(x4_hi_done, c * DK + (j + 1))
                v.tensor_tensor(x4[:, (2 * j + 1) * CH:(j + 1) * 2 * CH], x4_ps[j % 2], x4[:, j * 2 * CH:(2 * j + 1) * CH],
                                ALU.subtract).then_inc(x4_lo_done, 1)

            def weights_of(c, rows):
                for i in range(CT):
                    dve.wait_ge(gathered[i], c * 16 + 16)
                    ins = v.tensor_copy(cw_chunk[:, i * NE:(i + 1) * NE], rows[i][:, D:])
                ins.then_inc(cw_copied, 1)

            def piece_lo(e, j, split):
                hi, lo = split
                s = j % STAGES
                dve.wait_ge(w_hi_done, e * PIECES + (2 * PIECES + j + 1))
                v.scalar_tensor_tensor(lo[:, j * D:(j + 1) * D], stage[:, s * D:(s + 1) * D], WSCALE,
                                       hi[:, j * D:(j + 1) * D], ALU.mult, ALU.subtract).then_inc(e_lo_done, 1)

            for j in range(EARLY):
                piece_lo(0, j, (e_hi[1], e_lo[1]))
            weights_of(0, gx0)
            for j in range(DK):
                turned(0, j)

            def chunk(c, e, h, split, first=False):
                st4.enter(c * LINKS4)
                if split is not None and not first:
                    for j in range(EARLY):
                        piece_lo(e, j, split)
                for f in range(FK):
                    fs = slice(f * CH, (f + 1) * CH)
                    dve.wait_ge(gelu_done, c * FK + (FK + f + 1))
                    st4.link(v.tensor_copy(y_hi[:, fs], y32[:, fs]))
                    v.tensor_tensor(y_lo[:, fs], y32[:, fs], y_hi[:, fs], ALU.subtract).then_inc(y_lo_done, 1)
                dve.wait_ge(cw_copied, c + 1)
                dve.wait_ge(rows_added, c + 1)
                turned(c + 1, 0)
                turned(c + 1, 1)
                for i in range(CT):
                    for n in range(2):
                        k = 2 * i + n
                        o = y_out[i][:, n * HALF:(n + 1) * HALF]
                        dve.wait_ge(down_done, c * (2 * CT) + (k + 2))
                        ins = v.scalar_tensor_tensor(o, down_ps[n], 1.0 / WSCALE, b2_row[h][:, n * HALF:(n + 1) * HALF],
                                                     ALU.mult, ALU.add)
                        ins.then_inc(down_read, 1)
                        dve.wait_ge(down_read, c * (2 * CT) + (k + 3))
                        ins = v.tensor_scalar(o, o, cw_chunk[:, ds(i * NE + e, 1)], None, ALU.mult)
                        if n:
                            ins.then_inc(y_ready, 1)
                        turned(c + 1, k + 2)
                        if split is not None and 1 <= k <= PIECES - EARLY:
                            piece_lo(e, EARLY + k - 1, split)
                dve.wait_ge(y_ready, c * CT + CT)
                v.tensor_copy(hold[:, 1:2], hold[:, 0:1]).then_inc(y_ready_b2, 1)
                weights_of(c + 1, gx)

            LINKS4 = FK

            def expert(e, h, pair, split, first=False):
                c0 = dve.value_load(ranges2[0:1, 0, ds(e, 1)], min_val=0, max_val=MAXC - 3)
                c1 = dve.value_load(ranges2[0:1, 1, ds(e, 1)], min_val=1, max_val=MAXC - 2)
                more = dve.value_load(ranges2[0:1, 3, ds(e, 1)], min_val=0, max_val=1)
                dve.wait_ge(b2_in[h], pair * 16 + 16)
                chunk(0 if first else c0, e, h, split, first)
                with dve.If(more):
                    with dve.Fori(c0 + 1, c1) as c:
                        chunk(c, e, h, None)

            dve.wait_ge(ranges2_done, 1)
            expert(0, 0, 0, (e_hi[1], e_lo[1]), True)
            expert(1, 1, 0, (e_hi[0], e_lo[0]))
            with dve.Fori(1, NE // 2 - 1) as pair:
                for h in range(2):
                    expert(pair * 2 + h, h, pair, (e_hi[1 - h], e_lo[1 - h]))
            expert(NE - 2, 0, NE // 2 - 1, (e_hi[1], e_lo[1]))
            expert(NE - 1, 1, NE // 2 - 1, None)

            st5 = Steps(dve, dve_step5)
            for n, tiles in enumerate(LAST_GROUPS):
                cs = slice(tiles[0], tiles[-1] + 1)
                for r in tiles:
                    dve.wait_ge(fin_in[r], 16)
                    st5.did(v.bn_stats(stats5[:, r, 0:6], fin[r][:, 0:HALF]))
                    st5.did(v.bn_stats(stats5[:, r, 6:12], fin[r][:, HALF:D]))
                st5.wait()
                for r in tiles:
                    st5.did(v.bn_aggr(mv5[:, r, :], stats5[:, r, :]))
                st5.wait()
                v.tensor_scalar(var5[:, cs], mv5[:, cs, 1], EPS2, None, ALU.add).then_inc(var5_done, 1)
                for r in tiles:
                    if r >= POOL_TILES:
                        st5.did(v.scalar_tensor_tensor(fin[r], fin[r], mv5[:, r, 0:1], lnw_row[:], ALU.subtract, ALU.mult))
                dve.wait_ge(std5_done, n + 1)
                dve.wait_ge(var5_done, n + 1)
                st5.link(v.reciprocal(rstd5[:, cs], std5[:, cs]))
                st5.link(newton(rstd5[:, cs], var5[:, cs], q5[:, cs], st5))
                v.scalar_tensor_tensor(shift5[:, cs], mv5[:, cs, 0], -1.0, rstd5[:, cs], ALU.mult, ALU.mult
                                       ).then_inc(rstd5_done, 1)
            dve.wait_ge(x1b_done, NT)
            for r in range(POOL_TILES, NT):
                rs = slice(r * D, (r + 1) * D)
                dve.wait_ge(scaled, r + 1)
                v.tensor_tensor(t[:, rs], t[:, rs], fin[r], ALU.add).then_inc(fin_added_dve, 1)

        @block.tensor
        def _(pe):
            mm = nc.tensor.matmul
            pe.wait_ge(consts_done, PE_CONSTS)
            pe.wait_ge(spans_cols, 1)
            for i, vv in enumerate((first_v, last_v)):
                for h in range(2):
                    ins = nc.tensor.transpose(misc_ps[:, (2 * i + h) * P:(2 * i + h + 1) * P], vv[:, h, :], ident[:])
            ins.then_inc(spans_tr, 1)
            pe.wait_ge(spans_n, 1)
            mm(misc_ps[0:1, 0:NT], span[0:NT, 5:6], tri[0:NT, 0:NT], start=True, stop=True)
            mm(misc_ps[0:1, 16:16 + NT], span[0:NT, 5:6], ident[0:NT, 0:NT], start=True, stop=True)
            mm(misc_ps[0:1, 32:32 + NT], span[0:NT, 3:4], ident[0:NT, 0:NT], start=True,
               stop=True).then_inc(spans_ps, 1)

            def transposed(out, rows):
                for j in range(DK):
                    for h in range(2):
                        ins = mm(out[:, j * P:(j + 1) * P], rows[:, h * D + j * P:h * D + (j + 1) * P], ident16[:],
                                 start=(h == 0), stop=(h == 1), skip_group_check=True)
                return ins

            def turn(m):
                pe.wait_ge(xs_done, m + 1)
                pe.wait_ge(xt_lo_done, m)
                transposed(xt_ps, xs).then_inc(xt_done, 1)

            def count_block(m):
                pe.wait_ge(count_lo_read, m)
                i0 = pe.value_load(ranges[0:1, 0, ds(m, 1)], min_val=0, max_val=NT * NSTEP)
                i1 = pe.value_load(ranges[0:1, 1, ds(m, 1)], min_val=1, max_val=NT * NSTEP)
                w0 = (NT - 1 - m) * P
                for lo in range(0, NP, HALF):
                    n = min(HALF, NP - lo)
                    mm(count_ps[:, lo:lo + n], ident16[:], eye_wide[:, ds(w0 + lo, n)], start=True, stop=False,
                       skip_group_check=True)
                with pe.Fori(i0, i1) as i:
                    for u in range(GROUP):
                        if u % SUB == 0:
                            pe.wait_ge(onehot_done, i * (GROUP // SUB) + (u // SUB + 1))
                        for lo in range(0, NP, HALF):
                            n = min(HALF, NP - lo)
                            ins = mm(count_ps[:, lo:lo + n], onehots[:, u * OHW + NP:(u + 1) * OHW],
                                     onehots[:, u * OHW + lo:u * OHW + lo + n], start=False, stop=False,
                                     skip_group_check=True)
                        if u % SUB == SUB - 1:
                            ins.then_inc(onehot_used, 1)
                for lo in range(0, NP, HALF):
                    ins = mm(count_ps[:, lo:lo + P], zeros16[:], zeros16[:], start=False, stop=True,
                             skip_group_check=True)
                ins.then_inc(count_done, 1)

            def linear(m, halves=(0, 1)):
                pe.wait_ge(xt_lo_done, m + 1)
                if halves == (0, 1):
                    pe.wait_ge(lin_read, m)
                for n in halves:
                    for k in range(DK):
                        if halves == (0,):
                            pe.wait_ge(w_lo_done, k + 1)
                        x_hi = xt[:, ds((m % 2) * 2 * D + k * P, P)]
                        x_lo = xt[:, ds((m % 2) * 2 * D + D + k * P, P)]
                        ws = slice(k * D + n * HALF, k * D + (n + 1) * HALF)
                        o = lin_ps[:, n * HALF:(n + 1) * HALF]
                        mm(o, x_hi, w_hi[:, ws], start=(k == 0), stop=False)
                        mm(o, x_hi, w_lo[:, ws], start=False, stop=False)
                        ins = mm(o, x_lo, w_hi[:, ws], start=False, stop=(k == DK - 1))
                if halves != (0,):
                    ins.then_inc(lin_done, 1)

            pe.wait_ge(ranges_done, 1)
            pe.wait_ge(consts_done, ALL_CONSTS)
            turn(0)
            count_block(0)
            linear(0, (0,))
            count_block(1)
            turn(1)
            linear(0, (1,))
            with pe.Fori(1, NT - 1) as m:
                count_block(m + 1)
                turn(m + 1)
                linear(m)

            pe.wait_ge(count_hi_read, NT)
            for r in range(NT):
                for m in range(NT):
                    cs = slice(m * NP + r * P, m * NP + (r + 1) * P)
                    ins = mm(misc_ps[:, r:r + 1], ct_hi[:, cs], ones16[:, 0:1], start=(m == 0), stop=(m == NT - 1),
                             skip_group_check=True)
            ins.then_inc(deg_hi_done, 1)
            pe.wait_ge(over_cols, 1)
            mm(misc_ps[0:1, 16:16 + NT], ones16[:, 0:1], over[:], start=True, stop=True).then_inc(over_ps, 1)
            pe.wait_ge(over_done, 1)
            big_counts = pe.value_load(over_i[0:1, 0:1], min_val=0, max_val=P)
            mm(deg_lo_ps, zeros16[:], zeros16[:, 0:NT], start=True, stop=False, skip_group_check=True)
            with pe.If(big_counts):
                pe.wait_ge(count_lo_done, NT)
                for r in range(NT):
                    for m in range(NT):
                        cs = slice(m * NP + r * P, m * NP + (r + 1) * P)
                        mm(deg_lo_ps[:, r:r + 1], ct_lo[:, cs], ones16[:, 0:1], start=False, stop=False,
                           skip_group_check=True)
            mm(deg_lo_ps, zeros16[:], zeros16[:, 0:NT], start=False, stop=True, skip_group_check=True).then_inc(deg_done, 1)
            linear(NT - 1)

            def aggregate(r, n):
                o = agg_ps[r % 2][:, n * HALF:(n + 1) * HALF]
                if r >= 2:
                    pe.wait_ge(var_done, NT + r - 1)
                for m in range(NT):
                    cs = slice(m * NP + r * P, m * NP + (r + 1) * P)
                    at = m * 2 * D + n * HALF
                    if r == 0:
                        pe.wait_ge(hs_lo_done, m + 1)
                    mm(o, ct_hi[:, cs], hs[:, at:at + HALF], start=(m == 0), stop=False, skip_group_check=True)
                    mm(o, ct_hi[:, cs], hs[:, D + at:D + at + HALF], start=False, stop=False, skip_group_check=True)
                with pe.If(big_counts):
                    for m in range(NT):
                        cs = slice(m * NP + r * P, m * NP + (r + 1) * P)
                        at = m * 2 * D + n * HALF
                        mm(o, ct_lo[:, cs], hs[:, at:at + HALF], start=False, stop=False, skip_group_check=True)
                mm(o[:, 0:P], zeros16[:], zeros16[:], start=False, stop=True, skip_group_check=True).then_inc(agg_done, 1)

            def turn2(r):
                pe.wait_ge(xs_done, NT + r + 1)
                pe.wait_ge(x2t_lo_done, r)
                transposed(x2t_ps, xs).then_inc(x2t_done, 1)

            def route(r):
                pe.wait_ge(x2t_lo_done, r + 1)
                pe.wait_ge(mask_done, r)
                if r == 0:
                    pe.wait_ge(rw_lo_done, 1)
                o = router_ps[:, 0:NE]
                for k in range(DK):
                    hi, lo, ws = slice(k * P, (k + 1) * P), slice(D + k * P, D + (k + 1) * P), slice(k * NE, (k + 1) * NE)
                    mm(o, x2t[:, hi], rw_hi[:, ws], start=(k == 0), stop=False)
                    mm(o, x2t[:, hi], rw_lo[:, ws], start=False, stop=False)
                    ins = mm(o, x2t[:, lo], rw_hi[:, ws], start=False, stop=(k == DK - 1))
                ins.then_inc(router_done, 1)

            def rank(r):
                pe.wait_ge(mask_done, r + 1)
                pe.wait_ge(slots_done, r)
                mm(rank_ps[:, 0:NE], tri16[:], mask[:], start=True, stop=True)
                ins = mm(rank_ps[:, NE:2 * NE], ones16[:], mask[:], start=True, stop=True)
                if r == NT - 1:
                    v = N - r * P
                    ins = mm(rank_ps[:, 2 * NE:3 * NE], ones16[0:v, :], mask[0:v, :], start=True, stop=True)
                ins.then_inc(rank_done, 1)

            pe.wait_ge(count_lo_done, NT)
            for r in range(NT + 2):
                if r < NT:
                    aggregate(r, 0)
                if r >= 2:
                    route(r - 2)
                if r < NT:
                    aggregate(r, 1)
                if 1 <= r <= NT:
                    turn2(r - 1)
                if r >= 2:
                    rank(r - 2)

            pe.sem_inc(down_done, 1)
            def turn4(c, j, rows=gx):
                pe.wait_ge(x4_lo_done, c * DK + (j + 1))
                for i in range(CT):
                    if j == 0:
                        pe.wait_ge(gathered[i], c * 16 + 16)
                    for h in range(2):
                        ins = mm(x4_ps[j % 2][:, i * P:(i + 1) * P], rows[i].bitcast(F16)[:, h * D + j * P:h * D + (j + 1) * P],
                                 ident16[:], start=(h == 0), stop=(h == 1), skip_group_check=True)
                ins.then_inc(x4_done, 1)

            def up(c, w_hi, w_lo, turning):
                for js in [(j,) for j in range(DK - 2)] + [(DK - 2, DK - 1)]:
                    for j in js:
                        pe.wait_ge(x4_lo_done, c * DK + (j + 3))
                    for f in range(FK):
                        for j in js:
                            ws = slice(j * FF + f * P, j * FF + (f + 1) * P)
                            x_hi, x_lo = x4[:, j * 2 * CH:(2 * j + 1) * CH], x4[:, (2 * j + 1) * CH:(j + 1) * 2 * CH]
                            mm(up_ps[f], w_hi[:, ws], x_hi, start=(j == 0), stop=False)
                            mm(up_ps[f], w_hi[:, ws], x_lo, start=False, stop=False)
                            ins = mm(up_ps[f], w_lo[:, ws], x_hi, start=False, stop=(j == DK - 1))
                        if js[-1] == DK - 1:
                            ins.then_inc(up_done, 1)
                    if turning and js[0] + 2 < DK:
                        turn4(c, js[0] + 2, gx0)

            def down(c, w_hi, w_lo):
                turn4(c + 1, 0)
                turn4(c + 1, 1)
                for i in range(CT):
                    for n in range(2):
                        k = 2 * i + n
                        pe.wait_ge(down_read, c * (2 * CT) + (k + 1))
                        for f in range(FK):
                            if k == 0:
                                pe.wait_ge(y_lo_done, c * FK + (f + 1))
                            ys = slice(f * CH + i * P, f * CH + (i + 1) * P)
                            ws = slice(W2AT + f * D + n * HALF, W2AT + f * D + (n + 1) * HALF)
                            mm(down_ps[n], y_hi[:, ys], w_hi[:, ws], start=(f == 0), stop=False)
                            mm(down_ps[n], y_hi[:, ys], w_lo[:, ws], start=False, stop=False)
                            ins = mm(down_ps[n], y_lo[:, ys], w_hi[:, ws], start=False, stop=(f == FK - 1))
                        ins.then_inc(down_done, 1)
                        turn4(c + 1, k + 2)

            def chunks(c0, c1, e, h):
                with pe.Fori(c0, c1) as c:
                    pe.wait_ge(gelu_done, c * FK + FK)
                    up(c, e_hi[h], e_lo[h], False)
                    if not isinstance(e, int) or e:
                        pe.wait_ge(e_lo_done, e * PIECES)
                    down(c, e_hi[h], e_lo[h])

            def expert(e, h):
                c0 = pe.value_load(ranges2[0:1, 0, ds(e, 1)], min_val=0, max_val=MAXC - 3)
                c1 = pe.value_load(ranges2[0:1, 1, ds(e, 1)], min_val=1, max_val=MAXC - 2)
                pe.wait_ge(e_lo_done, e * PIECES - FK)
                settle(pe)
                chunks(c0, c1, e, h)

            pe.wait_ge(slots_done, NT)
            turn4(0, 0, gx0)
            turn4(0, 1, gx0)
            pe.wait_ge(w_lo_done, 2 * PIECES)
            up(0, e_hi[0], e_lo[0], True)
            down(0, e_hi[0], e_lo[0])
            pe.wait_ge(ranges2_done, 1)
            more = pe.value_load(ranges2[0:1, 3, 0:1], min_val=0, max_val=1)
            end = pe.value_load(ranges2[0:1, 1, 0:1], min_val=1, max_val=MAXC - 2)
            with pe.If(more):
                chunks(1, end, 0, 0)
            expert(1, 1)
            with pe.Fori(1, NE // 2) as pair:
                for h in range(2):
                    expert(pair * 2 + h, h)


def kernel(x, src, dst, L0_gnn_W, L0_gnn_b, L0_ffn_router_w, L0_ffn_router_b, L0_ffn_w1, L0_ffn_b1, L0_ffn_w2,
           L0_ffn_b2, L0_ffn_ln_w, L0_ffn_ln_b):
    import numpy as np
    import concourse.bacc as bacc
    from concourse.bass_utils import run_bass_kernel_spmd

    x = np.asarray(x)
    xp = np.zeros((NP, D), np.float32)
    xp[:N] = x
    src, dst = np.asarray(src), np.asarray(dst)
    wst = np.zeros((NE + 1, PIECES, P, D), np.float32)
    wst[0] = np.asarray(L0_gnn_W).T.reshape(PIECES, P, D)
    w1 = np.asarray(L0_ffn_w1).transpose(0, 2, 1).reshape(NE, DK // 2, 2, P, FF)
    wst[1:, :DK // 2] = w1.transpose(0, 1, 3, 2, 4).reshape(NE, DK // 2, P, D)
    wst[1:, DK // 2:] = np.asarray(L0_ffn_w2).transpose(0, 2, 1).reshape(NE, FK, P, D)
    arrays = {
        "x": xp,
        "src": np.ascontiguousarray(src.reshape(ET, EP).T),
        "dst": np.ascontiguousarray(dst.reshape(ET, EP).T),
        "dst_rows": np.ascontiguousarray(dst.reshape(ET, EP)),
        "wst": wst,
        "b": np.ascontiguousarray(np.asarray(L0_gnn_b)),
        "router_w": np.ascontiguousarray(np.asarray(L0_ffn_router_w).reshape(NE, DK, P).transpose(2, 1, 0)
                                         .reshape(P, DK * NE)),
        "router_b": np.ascontiguousarray(np.asarray(L0_ffn_router_b)),
        "b1": np.ascontiguousarray(np.asarray(L0_ffn_b1).reshape(NE * FK, P).T),
        "b2": np.ascontiguousarray(np.asarray(L0_ffn_b2)),
        "ln_w": np.ascontiguousarray(np.asarray(L0_ffn_ln_w)),
        "ln_b": np.ascontiguousarray(np.asarray(L0_ffn_ln_b)),
    }
    nc = bacc.Bacc("TRN2", target_bir_lowering=False, num_devices=1)
    args = {k: nc.dram_tensor(k + "_in", a.shape, mybir.dt.from_np(a.dtype), kind="ExternalInput").ap()
            for k, a in arrays.items()}
    y = nc.dram_tensor("out_dram", (NP, D), F32, kind="ExternalOutput").ap()
    scratch = {
        "x2_rows": nc.dram_tensor("x2_rows", (NROW, XW), F32).ap(),
        "acc_rows": nc.dram_tensor("acc_rows", (NROW, D), F32).ap(),
        "slot_table": nc.dram_tensor("slot_table", (NE * CAP, 1), I32).ap(),
    }
    build(nc, **args, **scratch, out=y)
    r = run_bass_kernel_spmd(nc, [{k + "_in": a for k, a in arrays.items()}], core_ids=[0])
    return r.results[0]["out_dram"][:N]
```

```python
from contextlib import ExitStack

import concourse.bass as bass
from concourse import mybir
from concourse.alu_op_type import AluOpType as ALU

F32 = mybir.dt.float32
F16 = mybir.dt.float16
F8 = mybir.dt.float8e4
I32 = mybir.dt.int32
U32 = mybir.dt.uint32
ACT = mybir.ActivationFunctionType
AXX = mybir.AxisListType.X
ds = bass.ds

P = 128
N = 1250
NT = -(-N // P)
NP = NT * P
D = 1024
DK = D // P
HALF = 512
E = 20000
EP = P
ET = -(-E // EP)
BIG = 1000.0
NE = 8
FF = 512
FK = FF // P
PIECES = 8
STAGES = 4
RING = 9
MAIN = 2 * RING - 1
EXTRA = 2
ETP = ET + MAIN + EXTRA
NSTEP = -(-(ET - MAIN) // EXTRA)
SPLIT = 1024
OHW = NP + P
WSCALE = 256.0
EPS1 = 1e-5
EPS2 = 1e-12
CT = 3
CH = CT * P
CPE = -(-N // CH)
CAP = CPE * CH
NROW = NP + CH
MAXC = NE + 2 * N // CH + 2
EXACT16 = 2048.0
RANGE_CONSTS, PE_CONSTS, EDGE_CONSTS, ALL_CONSTS = 4, 7, 8, 15
LAST_GROUPS = (0, 1, 2, 3), (4, 5, 6, 7), (8, 9)
ACT_TILES = (0, 1), (4, 5)
WIDTHS = 296, 312, 336, CH
CPT = CAP // P
FIRST = 0, 1
FIRST_CH = len(FIRST) * P
FIRST_TILES = 7
PLAN = 32
EARLY = 4
W2AT = DK * FF


class Steps:

    def __init__(self, eng, sem):
        self.eng, self.sem, self.base, self.k = eng, sem, 0, 0

    def enter(self, base):
        self.base, self.k = base, 0

    def did(self, ins):
        self.k += 1
        ins.then_inc(self.sem, 1)

    def wait(self):
        self.eng.wait_ge(self.sem, self.base + self.k)

    def link(self, ins):
        self.did(ins)
        self.wait()


def build(nc, x, src, dst, dst_rows, wst, b, router_w, router_b, b1, b2, ln_w, ln_b,
          x2_rows, cw_rows, acc_rows, slot_table, out):
    ctx = ExitStack()
    with ctx:
        def sb(name, shape, dt):
            return ctx.enter_context(nc.sbuf_tensor(name, shape, dt))

        def sem(name):
            return ctx.enter_context(nc.semaphore(name))

        early = sb("early", [P, CT * D], F32)
        iota16 = early[:, 0:NP // 2].bitcast(F16)
        at = NP // 2
        zeros16 = early[:, at:at + P // 2].bitcast(F16)
        at += P // 2
        zero_row = early[:, at:at + D]
        at += D
        ct_lo_16 = early[:, at:at + NP // 2].bitcast(F16)
        at += NP // 2
        ct_lo_8 = early[:, at:at + NP // 4].bitcast(F8)
        assert at + NP // 4 <= CT * D
        gx0 = [early[:, i * D:(i + 1) * D] for i in range(CT)]
        ident = sb("ident", [P, P], F32)
        ident16 = sb("ident16", [P, P], F16)
        ones16 = sb("ones16", [P, P], F16)
        tri = sb("tri", [P, NT], F32)
        tri16 = sb("tri16", [P, P], F16)
        block_lo = sb("block_lo", [P, NT], F32)
        block_hi = sb("block_hi", [P, NT], F32)
        tile_no = sb("tile_no", [P, 2], F32)
        b_row = sb("b_row", [P, D], F32)
        src_i = sb("src_i", [EP, ET], I32)
        dst_i = sb("dst_i", [EP, ET], I32)
        src_f = sb("src_f", [EP, ETP], F32)
        dst_f = sb("dst_f", [EP, ETP], F32)
        tile_min = sb("tile_min", [P, 2], F32)
        tile_max = sb("tile_max", [P, 2], F32)
        overlap = sb("overlap", [P, 2, 16], F32)
        tile_from = sb("tile_from", [P, 2], F32)
        tile_to = sb("tile_to", [P, 2], F32)
        span = sb("span", [P, 8], F32)
        span_row = sb("span_row", [1, 64], F32)
        steps_f = sb("steps_f", [1, NT], F32)
        ranges = sb("ranges", [1, 2, 16], I32)
        t = sb("t", [P, NT * D], F32)
        stage = sb("stage", [P, STAGES * D], F32)
        wbuf0 = sb("wbuf0", [P, 2 * PIECES * D], F16)
        wbuf1 = sb("wbuf1", [P, 2 * NT * D], F16)
        counts = sb("counts", [P, NT * NP * 3 // 4], F32)
        ct_hi = counts[:, 0:NT * NP // 2].bitcast(F16)
        ct_lo = counts[:, NT * NP // 2:].bitcast(F8)
        step_from = counts[:, 0:NSTEP]
        steps_in = counts[:, NSTEP:2 * NSTEP]
        work = sb("work", [P, CT * D], F32)
        xn = work[:, 0:D]
        x2t = work[:, D:2 * D].bitcast(F16)
        xs = work[:, 2 * D:3 * D].bitcast(F16)
        first_v = work[:, D:D + 2 * P].rearrange("p (h k) -> p h k", h=2)
        last_v = work[:, D + 2 * P:D + 4 * P].rearrange("p (h k) -> p h k", h=2)
        at = D + 4 * P
        dst_r = work[:, at:at + 2 * EP].bitcast(I32).rearrange("p (h k) -> p h k", h=2)
        at += 2 * EP
        dst_rf = work[:, at:at + 2 * EP].rearrange("p (h k) -> p h k", h=2)
        assert at + 2 * EP <= 2 * D
        stats = sb("stats", [P, 12], F32)
        mv = sb("mv", [P, 2], F32)
        std = sb("std", [P, 2], F32)
        rstd = sb("rstd", [P, 1], F32)
        q_col = sb("q_col", [P, 1], F32)
        deg_s = sb("deg_s", [P, NT], F32)
        deg_f = sb("deg_f", [P, NT], F32)
        q_dis = sb("q_dis", [P, NT], F32)
        dis = sb("dis", [P, NT], F32)
        over = sb("over", [P, NT], F16)
        over_row = sb("over_row", [1, 4], F32)
        over_i = sb("over_i", [1, 4], I32)
        hold = sb("hold", [P, 2], F32)
        expert_no = sb("expert_no", [P, NE], F32)
        token_no = sb("token_no", [P, NT], I32)
        slot_ids = sb("slot_ids", [P, NE * CPE * CT], I32)
        rw = sb("rw", [P, DK * NE], F32)
        rw_hi = sb("rw_hi", [P, DK * NE], F16)
        rw_lo = sb("rw_lo", [P, DK * NE], F16)
        rb_row = sb("rb_row", [P, NE], F32)
        lnw_row = sb("lnw_row", [P, D], F32)
        logits = sb("logits", [P, NE], F32)
        top = sb("top", [P, 8], F32)
        top_i = sb("top_i", [P, 8], U32)
        top_f = sb("top_f", [P, 2], F32)
        oh = sb("oh", [P, 2 * NE], F32)
        oh_all = sb("oh_all", [P, NT * 2 * NE], F32)
        mask = sb("mask", [P, NE], F16)
        gap = sb("gap", [P, NT], F32)
        carry = sb("carry", [P, NE], F32)
        slot_of = sb("slot_of", [P, NE], F32)
        slot_pick = sb("slot_pick", [P, 2 * NE], F32)
        slot_f = sb("slot_f", [P, 2], F32)
        slot_m = sb("slot_m", [P, 2], F32)
        slot_i = sb("slot_i", [P, 2], I32)
        slots = sb("slots", [P, NT * 2], I32)
        out_no = slots[:, 0:NT]
        cnt = sb("cnt", [1, NE], F32)
        scan = sb("scan", [1, 4, 2 * NE], F32)
        first_slot = sb("first_slot", [P, NE], F32)
        ranges2_f = sb("ranges2_f", [1, 4, NE], F32)
        ranges2 = sb("ranges2", [1, 4, NE], I32)
        last_chunk = sb("last_chunk", [1, 1], I32)
        last_ends = sb("last_ends", [1, NT], F32)
        last_base = sb("last_base", [1, 1], F32)
        needs_f = sb("needs_f", [1, NT], F32)
        needs = sb("needs", [1, NT], I32)
        plans_f = sb("plans_f", [1, NE], F32)
        plans = sb("plans", [1, NE], I32)
        chunk_i = sb("chunk_i", [1, MAXC], F32)
        chunk_skip = sb("chunk_skip", [1, MAXC, NE], F32)
        chunk_f = sb("chunk_f", [1, MAXC], F32)
        chunk_at = sb("chunk_at", [1, MAXC], I32)
        gap_e = sb("gap_e", [P, NT], F32)
        wt = sb("wt", [P, 2 * NT], F32)
        cw = sb("cw", [P, NT * NE], F32)
        cw2 = sb("cw2", [P, NT * NE], F32)
        b1t = sb("b1t", [P, NE * FK], F32)
        ids = sb("ids", [P, CT], I32)
        ids_out = sb("ids_out", [P, CT], I32)
        ids_first = sb("ids_first", [P, len(FIRST)], I32)
        cw_next = sb("cw_next", [P, CT * NE], F32)
        cw_chunk = sb("cw_chunk", [P, CT * NE], F32)
        gx = [counts[:, i * D:(i + 1) * D] for i in range(CT)]
        at = CT * D
        x4 = counts[:, at:at + DK * CH].bitcast(F16)
        at += DK * CH
        y32 = counts[:, at:at + FK * CH]
        at += FK * CH
        y_hi = counts[:, at:at + FK * CH // 2].bitcast(F16)
        at += FK * CH // 2
        y_lo = counts[:, at:at + FK * CH // 2].bitcast(F16)
        assert at + FK * CH // 2 <= NT * NP * 3 // 4
        y_out = [work[:, i * D:(i + 1) * D] for i in range(CT)]
        b2_row = [wbuf1[:, 2 * PIECES * D + i * 2 * D:2 * PIECES * D + (i + 1) * 2 * D].bitcast(F32) for i in range(2)]
        fin = [wbuf0[:, r * 2 * D:(r + 1) * 2 * D].bitcast(F32) if r < PIECES
               else stage[:, (r - PIECES) * D:(r - PIECES + 1) * D] for r in range(NT)]
        stats5 = oh_all[:, 0:NT * 12].rearrange("p (r s) -> p r s", s=12)
        mv5 = cw2[:, 0:2 * NT].rearrange("p (r s) -> p r s", s=2)
        sum5, minus5, square5 = [cw[:, i * NT:(i + 1) * NT] for i in range(3)]
        var5, std5, rstd5, q5 = [cw2[:, (2 + i) * NT:(3 + i) * NT] for i in range(4)]
        e_hi = [w[:, 0:PIECES * D] for w in (wbuf0, wbuf1)]
        e_lo = [w[:, PIECES * D:2 * PIECES * D] for w in (wbuf0, wbuf1)]

        onehots = wbuf1[:, 0:(RING + EXTRA) * OHW]
        XT_AT = 2 * (NT - 2) * D
        assert (RING + EXTRA) * OHW <= XT_AT
        xt = wbuf1[:, XT_AT:]
        w_hi, w_lo = e_hi[0], e_lo[0]
        hs = wbuf1[:]

        ps = ctx.enter_context(nc.psum_tensor("ps", [P, 8 * HALF], F32))

        def bank(i, n=1):
            return ps[:, i * HALF:(i + n) * HALF]

        count_ps = ps[:, 0:NP]
        xt_ps = bank(3, 2)
        lin_ps = bank(5, 2)
        misc_ps = bank(7)
        deg_lo_ps = misc_ps[:, 48:48 + NT]
        agg_ps = [bank(0, 2), bank(2, 2)]
        x2t_ps = bank(4, 2)
        router_ps = bank(6)
        rank_ps = bank(7)
        up_ps = [ps[:, c * HALF:c * HALF + CH] for c in range(FK)]
        x4_ps = [ps[:, (4 + i) * HALF:(4 + i) * HALF + CH] for i in range(2)]
        down_ps = [bank(6), bank(7)]

        act_step5 = sem("act_step5")
        agg_done = sem("agg_done")
        b_in = sem("b_in")
        blank = sem("blank")
        chunks_done = sem("chunks_done")
        consts_done = sem("consts_done")
        consts_in = sem("consts_in")
        count_done = sem("count_done")
        count_hi_read = sem("count_hi_read")
        count_lo_8 = sem("count_lo_8")
        count_lo_done = sem("count_lo_done")
        count_lo_read = sem("count_lo_read")
        cw_copied = sem("cw_copied")
        cw_done = sem("cw_done")
        cw_in = sem("cw_in")
        cw_stored = sem("cw_stored")
        deg_done = sem("deg_done")
        deg_hi_done = sem("deg_hi_done")
        deg_sqrt = sem("deg_sqrt")
        deg_summed = sem("deg_summed")
        dis_done = sem("dis_done")
        down_done = sem("down_done")
        down_read = sem("down_read")
        dst_rows_in = sem("dst_rows_in")
        dve_step = sem("dve_step")
        dve_step3 = sem("dve_step3")
        dve_step4 = sem("dve_step4")
        dve_step5 = sem("dve_step5")
        e_lo_done = sem("e_lo_done")
        edges_in = sem("edges_in")
        first_done = sem("first_done")
        first_hi_done = sem("first_hi_done")
        first_lo_done = sem("first_lo_done")
        gap_done = sem("gap_done")
        gap_exp = sem("gap_exp")
        gelu_done = sem("gelu_done")
        hs_hi_done = sem("hs_hi_done")
        hs_lo_done = sem("hs_lo_done")
        ids_in = sem("ids_in")
        last_adds = sem("last_adds")
        lin_done = sem("lin_done")
        lin_read = sem("lin_read")
        lnb_in = sem("lnb_in")
        mask_done = sem("mask_done")
        needs_done = sem("needs_done")
        onehot_done = sem("onehot_done")
        onehot_used = sem("onehot_used")
        out_added = sem("out_added")
        out_no_done = sem("out_no_done")
        out_stored = sem("out_stored")
        over_cols = sem("over_cols")
        over_done = sem("over_done")
        over_ps = sem("over_ps")
        plans_done = sem("plans_done")
        pool_step4 = sem("pool_step4")
        ranges2_done = sem("ranges2_done")
        ranges_done = sem("ranges_done")
        rank_done = sem("rank_done")
        router_done = sem("router_done")
        rows_added = sem("rows_added")
        rstd5_done = sem("rstd5_done")
        rw_hi_done = sem("rw_hi_done")
        rw_lo_done = sem("rw_lo_done")
        scaled = sem("scaled")
        scattered = sem("scattered")
        scattered_first = sem("scattered_first")
        slots_done = sem("slots_done")
        spans_cols = sem("spans_cols")
        spans_n = sem("spans_n")
        spans_ps = sem("spans_ps")
        spans_tr = sem("spans_tr")
        spare_in = sem("spare_in")
        square5_done = sem("square5_done")
        std5_done = sem("std5_done")
        std_done = sem("std_done")
        table_in = sem("table_in")
        table_loaded = sem("table_loaded")
        up_done = sem("up_done")
        var5_done = sem("var5_done")
        var_done = sem("var_done")
        w_hi_done = sem("w_hi_done")
        w_lo_done = sem("w_lo_done")
        w_scaled = sem("w_scaled")
        weighed = sem("weighed")
        x0_in = sem("x0_in")
        x1_in = sem("x1_in")
        x1b_done = sem("x1b_done")
        x2_first_stored = sem("x2_first_stored")
        x2_stored = sem("x2_stored")
        x2t_done = sem("x2t_done")
        x2t_hi_done = sem("x2t_hi_done")
        x2t_lo_done = sem("x2t_lo_done")
        x4_done = sem("x4_done")
        x4_hi_done = sem("x4_hi_done")
        x4_lo_done = sem("x4_lo_done")
        x_again0 = sem("x_again0")
        x_again1 = sem("x_again1")
        xn_done = sem("xn_done")
        xrest_in = sem("xrest_in")
        xs_done = sem("xs_done")
        xs_hi_done = sem("xs_hi_done")
        xt_done = sem("xt_done")
        xt_hi_done = sem("xt_hi_done")
        xt_lo_done = sem("xt_lo_done")
        y_lo_done = sem("y_lo_done")
        y_ready = sem("y_ready")
        y_ready_b2 = sem("y_ready_b2")
        carrier = sem("carrier")
        gathered = [sem(f"gathered{i}") for i in range(CT)]
        added = [sem(f"added{i}") for i in range(CT)]
        fin_in = [sem(f"fin_in{i}") for i in range(NT)]
        stage_in = [sem(f"stage_in{i}") for i in range(STAGES)]
        b2_in = [sem(f"b2_in{i}") for i in range(2)]

        def settle(eng):
            eng.sem_inc(carrier, 1)

        def stored(eng, r):
            eng.wait_ge(x2_first_stored, 16 * min(r, FIRST_TILES))
            eng.wait_ge(x2_stored, 16 * r + 16 * max(r - FIRST_TILES, 0))

        block = ctx.enter_context(nc.Block())

        @block.gpsimd
        def _(pool):
            g = nc.gpsimd
            for c in (g.iota(block_lo[:], [[P, NT]], base=0, channel_multiplier=0, allow_small_or_imprecise_dtypes=True),
                      g.iota(block_hi[:], [[P, NT]], base=P, channel_multiplier=0, allow_small_or_imprecise_dtypes=True),
                      g.iota(tile_no[:], [[P, 2]], base=0, channel_multiplier=1, allow_small_or_imprecise_dtypes=True),
                      g.iota(step_from[:], [[EXTRA, NSTEP]], base=MAIN, channel_multiplier=0,
                             allow_small_or_imprecise_dtypes=True),
                      g.memset(span[:], 0.0)):
                c.then_inc(consts_done, 1)
            pool.wait_ge(blank, 2)
            g.affine_select(out=ident[:], in_=ident[:], compare_op=ALU.not_equal, fill=1.0, base=0,
                            pattern=[[-1, P]], channel_multiplier=1).then_inc(consts_done, 1)
            g.affine_select(out=tri[:], in_=tri[:], compare_op=ALU.is_gt, fill=0.0, base=0,
                            pattern=[[1, NT]], channel_multiplier=-1).then_inc(consts_done, 1)
            g.iota(iota16[:], [[1, NP]], base=0, channel_multiplier=0,
                   allow_small_or_imprecise_dtypes=True).then_inc(consts_done, 1)
            pool.wait_ge(blank, 5)
            g.affine_select(out=ident16[:], in_=ident16[:], compare_op=ALU.not_equal, fill=1.0, base=0,
                            pattern=[[-1, P]], channel_multiplier=1).then_inc(consts_done, 1)
            g.affine_select(out=tri16[:], in_=tri16[:], compare_op=ALU.is_gt, fill=0.0, base=0,
                            pattern=[[1, P]], channel_multiplier=-1).then_inc(consts_done, 1)
            for c in (g.memset(ones16[:], 1.0),
                      g.iota(expert_no[:], [[1, NE]], base=0, channel_multiplier=0, allow_small_or_imprecise_dtypes=True),
                      g.iota(first_slot[:], [[CAP, NE]], base=0, channel_multiplier=0,
                             allow_small_or_imprecise_dtypes=True),
                      g.iota(chunk_i[:], [[1, MAXC]], base=0, channel_multiplier=0, allow_small_or_imprecise_dtypes=True),
                      g.iota(token_no[:], [[P, NT]], base=CH, channel_multiplier=1)):
                c.then_inc(consts_done, 1)
            g.iota(slot_ids[:], [[0, NE * CPE], [1, CT]], base=0, channel_multiplier=CT).then_inc(table_in, 1)
            g.memset(zero_row, 0.0).then_inc(spare_in, 1)

            def split_lo(q, hi, lo):
                s = q % STAGES
                cs = slice(q % PIECES * D, (q % PIECES + 1) * D)
                pool.wait_ge(w_hi_done, q + 1)
                g.tensor_tensor(lo[:, cs], stage[:, s * D:(s + 1) * D], hi[:, cs], ALU.subtract).then_inc(w_lo_done, 1)

            def xs_lo(m):
                pool.wait_ge(xs_hi_done, m + 1)
                g.tensor_tensor(xs[:, D:], xn, xs[:, 0:D], ALU.subtract).then_inc(xs_done, 1)

            def count_lo_8_copy(m):
                pool.wait_ge(count_lo_read, m + 1)
                settle(pool)
                g.tensor_copy(ct_lo_8[:], ct_lo_16[:], saturate=False).then_inc(count_lo_8, 1)
                pool.wait_ge(count_lo_8, m + 1)
                settle(pool)
                g.tensor_copy(ct_lo[:, ds(m * NP, NP)].bitcast(U32), ct_lo_8[:].bitcast(U32)).then_inc(count_lo_done, 1)

            for q in range(PIECES):
                split_lo(q, w_hi, w_lo)
                if q == 1:
                    xs_lo(0)
            xs_lo(1)
            count_lo_8_copy(0)
            with pool.Fori(1, NT - 1) as m:
                xs_lo(m + 1)
                count_lo_8_copy(m)
            count_lo_8_copy(NT - 1)

            def add_lnb(r):
                rs = slice(r * D, (r + 1) * D)
                pool.wait_ge(xn_done, NT + r + 1)
                g.tensor_tensor(t[:, rs], t[:, rs], b_row[:], ALU.add).then_inc(x1b_done, 1)

            def gather_first(i, ids, tiles):
                g.indirect_dma_start(out=gx0[i], out_offset=None, in_=x2_rows[0:CH + tiles * P, :],
                                     in_offset=bass.IndirectOffsetOnAxis(ap=ids[:, i:i + 1].bitcast(U32), axis=0)
                                     ).then_inc(gathered[i], 16)

            pool.wait_ge(lnb_in, 16)
            pool.wait_ge(consts_in, 16 * 5)
            for r in range(NT + 2):
                if r < NT - 1:
                    xs_lo(NT + r)
                if 2 <= r:
                    if r - 2 == FIRST_TILES:
                        pool.wait_ge(agg_done, 2 * NT)
                        pool.wait_ge(x2_first_stored, 16 * FIRST_TILES)
                        pool.wait_ge(ids_in, 16)
                        for i in FIRST:
                            gather_first(i, ids_first, FIRST_TILES)
                    pool.wait_ge(slots_done, r - 1)
                    for n in range(2):
                        c = 2 * (r - 2) + n
                        g.indirect_dma_start(out=slot_table, out_offset=bass.IndirectOffsetOnAxis(
                            ap=slots[:, c:c + 1].bitcast(U32), axis=0), in_=token_no[:, r - 2:r - 1],
                            in_offset=None).then_inc(scattered_first if r - 2 < FIRST_TILES else scattered, 16)
                if 2 <= r < NT:
                    split_lo(PIECES + r - 2, e_hi[0], e_lo[0])
                if 1 <= r < NT - 1:
                    add_lnb(r - 1)

            st4 = Steps(pool, pool_step4)

            def gather_weights():
                for i in range(CT):
                    g.indirect_dma_start(out=cw_next[:, i * NE:(i + 1) * NE], out_offset=None, in_=cw_rows,
                                         in_offset=bass.IndirectOffsetOnAxis(ap=ids[:, i:i + 1].bitcast(U32), axis=0)
                                         ).then_inc(cw_in, 16)

            def gather(rows):
                for i in range(CT):
                    g.indirect_dma_start(out=rows[i], out_offset=None, in_=x2_rows,
                                         in_offset=bass.IndirectOffsetOnAxis(ap=ids[:, i:i + 1].bitcast(U32), axis=0)
                                         ).then_inc(gathered[i], 16)

            def chunk_ids(c, into):
                no = pool.value_load(chunk_at[0:1, ds(c, 1)], min_val=0, max_val=NE * CPE - 1)
                st4.did(g.tensor_copy(into[:], slot_ids[:, ds(no * CT, CT)]))
                st4.wait()

            pool.wait_ge(x2_stored, 16 * NT + 16 * (NT - FIRST_TILES))
            pool.wait_ge(ids_in, 2 * 16)
            for i in range(len(FIRST), CT):
                gather_first(i, ids, NT)
            pool.wait_ge(cw_stored, 16)
            gather_weights()
            pool.wait_ge(table_loaded, 16)
            pool.wait_ge(chunks_done, 1)
            c_last = pool.value_load(last_chunk[:], min_val=NE - 1, max_val=MAXC - 3)

            def chunk(c, first, last=False):
                st4.enter(2 * c)
                if not last:
                    for i in range(CT):
                        pool.wait_ge(gathered[i], 16 * c + 16)
                    pool.wait_ge(cw_in, 16 * CT * (c + 1))
                    settle(pool)
                    chunk_ids(c + 1, ids)
                    if not first:
                        pool.wait_ge(x4_done, DK * c + DK)
                        settle(pool)
                    gather(gx)
                    pool.wait_ge(cw_copied, c + 1)
                    settle(pool)
                    gather_weights()
                if first:
                    add_lnb(NT - 2)
                    add_lnb(NT - 1)
                else:
                    for i in range(CT):
                        pool.wait_ge(added[i], 16 * c)
                    pool.sem_inc(rows_added, 1)
                if last:
                    pool.sem_inc(last_adds, 1)
                chunk_ids(c, ids_out)
                for i in range(CT):
                    pool.wait_ge(y_ready, CT * c + (i + 1))
                    settle(pool)
                    g.indirect_dma_start(out=acc_rows, out_offset=bass.IndirectOffsetOnAxis(
                        ap=ids_out[:, i:i + 1].bitcast(U32), axis=0), in_=y_out[i], in_offset=None,
                        compute_op=ALU.add).then_inc(added[i], 16)
                    if last:
                        pool.wait_ge(added[i], 16 * c + 16)
                        pool.sem_inc(last_adds, 1)

            chunk(0, True)
            with pool.Fori(1, c_last) as c:
                chunk(c, False)
            chunk(c_last, False, True)

            g.iota(out_no, [[P, NT]], base=0, channel_multiplier=1).then_inc(out_no_done, 1)
            pool.wait_ge(out_no_done, 1)
            pool.wait_ge(out_stored, 16 * NT)
            for r in range(NT):
                pool.wait_ge(scaled, r + 1)
                g.indirect_dma_start(out=out, out_offset=bass.IndirectOffsetOnAxis(
                    ap=out_no[:, r:r + 1].bitcast(U32), axis=0), in_=fin[r], in_offset=None,
                    compute_op=ALU.add).then_inc(out_added, 16)
            pool.wait_ge(out_added, 16 * NT)

        @block.sync
        def _(sp):
            def piece(q, splits):
                if splits:
                    sp.wait_ge(w_lo_done, q - STAGES + 1)
                s = q % STAGES
                sp.dma_start(stage[:, s * D:(s + 1) * D], wst[q // PIECES, q % PIECES]).then_inc(stage_in[s], 16)

            sp.dma_start(dst_r[:, 0, :], dst_rows[0:P, :]).then_inc(dst_rows_in, 16)
            sp.dma_start(dst_r[0:ET - P, 1, :], dst_rows[P:ET, :]).then_inc(dst_rows_in, 16)
            sp.dma_start(t[:, 0:D], x[0:P, :]).then_inc(x0_in, 16)
            sp.dma_start(src_i[:], src).then_inc(edges_in, 16)
            sp.dma_start(dst_i[:], dst).then_inc(edges_in, 16)
            for q in range(STAGES):
                piece(q, False)
            sp.dma_start(t[:, D:2 * D], x[P:2 * P, :]).then_inc(x1_in, 16)
            for q in range(STAGES, PIECES):
                piece(q, True)
            sp.dma_start(b_row[:], b.partition_broadcast(P)).then_inc(b_in, 16)
            sp.dma_start(t[:, 2 * D:].rearrange("p (r d) -> p r d", d=D),
                         x[2 * P:, :].rearrange("(r p) d -> p r d", p=P)).then_inc(xrest_in, 16)
            for q in range(PIECES, PIECES + STAGES):
                piece(q, True)
            for dst_ap, src_ap in ((rw[:], router_w), (rb_row[:], router_b.partition_broadcast(P)), (b1t[:], b1),
                                   (lnw_row[:], ln_w.partition_broadcast(P))):
                sp.dma_start(dst_ap, src_ap).then_inc(consts_in, 16)
            sp.wait_ge(table_in, 1)
            slot_table_v = slot_table.rearrange("(e p t) o -> p e (t o)", e=NE, p=P)
            slot_ids_v = slot_ids[:].rearrange("p (e t) -> p e t", e=NE)
            sp.dma_start(slot_table_v, slot_ids_v).then_inc(consts_in, 16)
            sp.wait_ge(spare_in, 1)
            for i in range(CT):
                rows = slice(i * P, (i + 1) * P)
                sp.dma_start(x2_rows[rows, :], zero_row).then_inc(spare_in, 16)
                sp.dma_start(cw_rows[rows, :], zero_row[:, 0:NE]).then_inc(spare_in, 16)
                sp.dma_start(acc_rows[rows, :], zero_row).then_inc(spare_in, 16)
            sp.wait_ge(hs_lo_done, 2)
            sp.dma_start(t[:, 0:2 * D].rearrange("p (r d) -> p r d", d=D),
                         x[0:2 * P, :].rearrange("(r p) d -> p r d", p=P)).then_inc(x_again0, 16)
            sp.wait_ge(lin_read, NT)
            sp.dma_start(b_row[:], ln_b.partition_broadcast(P)).then_inc(lnb_in, 16)
            sp.wait_ge(hs_lo_done, NT)
            sp.dma_start(t[:, 2 * D:].rearrange("p (r d) -> p r d", d=D),
                         x[2 * P:, :].rearrange("(r p) d -> p r d", p=P)).then_inc(x_again1, 16)
            for r in range(NT):
                rows = slice(CH + r * P, CH + (r + 1) * P)
                sp.wait_ge(xn_done, NT + r + 1)
                sp.dma_start(acc_rows[rows, :], xn).then_inc(x2_stored, 16)
                sp.wait_ge(xs_done, NT + r + 1)
                sp.dma_start(x2_rows[rows, :], xs.bitcast(F32)
                             ).then_inc(x2_first_stored if r < FIRST_TILES else x2_stored, 16)
                if r == FIRST_TILES + 1:
                    sp.wait_ge(scattered_first, 16 * 2 * FIRST_TILES)
                    sp.dma_start(ids_first[:], slot_table_v[:, 0, 0:len(FIRST)]).then_inc(ids_in, 16)
                if 2 <= r:
                    piece(PIECES + STAGES + r - 2, True)
            sp.wait_ge(cw_done, 1)
            sp.dma_start(cw_rows[CH:, :].rearrange("(r p) e -> p r e", p=P),
                         cw[:].rearrange("p (r e) -> p r e", e=NE)).then_inc(cw_stored, 16)
            sp.wait_ge(scattered, 16 * 2 * (NT - FIRST_TILES))
            sp.dma_start(ids[:], slot_table_v[:, 0, 0:CT]).then_inc(ids_in, 16)
            sp.dma_start(slot_ids_v, slot_table_v).then_inc(table_loaded, 16)
            pieces = wst.rearrange("i q p d -> (i q) p d")
            with sp.Fori(PIECES // STAGES * 2 + 1, (NE + 1) * PIECES // STAGES) as u:
                for s in range(STAGES):
                    sp.wait_ge(e_lo_done, u * STAGES + (s - STAGES + 1 - 2 * PIECES))
                    sp.dma_start(stage[:, s * D:(s + 1) * D], pieces[ds(u * STAGES + s, 1)].rearrange("o p d -> (o p) d")
                                 ).then_inc(stage_in[s], 16)
            sp.wait_ge(x1b_done, NT)
            for r in range(NT):
                sp.dma_start(out[r * P:(r + 1) * P, :], t[:, r * D:(r + 1) * D]).then_inc(out_stored, 16)
            sp.wait_ge(e_lo_done, (NE - 1) * PIECES)
            sp.wait_ge(needs_done, 1)
            for r in range(NT):
                sp.wait_ge(last_adds, sp.value_load(needs[0:1, r:r + 1], min_val=1, max_val=CT + 1))
                settle(sp)
                sp.dma_start(fin[r], acc_rows[CH + r * P:CH + (r + 1) * P, :]).then_inc(fin_in[r], 16)
            sp.wait_ge(out_stored, 16 * NT)

        @block.scalar
        def _(act):
            a = nc.scalar

            scaled_of = Steps(act, w_scaled)

            def split_hi(q, hi):
                s, j = q % STAGES, q % PIECES
                piece = stage[:, s * D:(s + 1) * D]
                act.wait_ge(stage_in[s], (q // STAGES) * 16 + 16)
                scaled_of.link(a.activation(piece, piece, ACT.Copy, scale=WSCALE))
                a.activation(hi[:, j * D:(j + 1) * D], piece, ACT.Copy).then_inc(w_hi_done, 1)

            def sqrt_var(n):
                act.wait_ge(var_done, n)
                a.activation(std[:, 1:2], std[:, 0:1], ACT.Sqrt).then_inc(std_done, 1)

            def xs_hi(m):
                act.wait_ge(xn_done, m + 1)
                act.wait_ge(xt_done, m)
                a.activation(xs[:, 0:D], xn, ACT.Copy).then_inc(xs_hi_done, 1)

            def count_hi(m):
                act.wait_ge(count_done, m + 1)
                settle(act)
                a.activation(ct_hi[:, ds(m * NP, NP)], count_ps, ACT.Copy).then_inc(count_hi_read, 1)

            def xt_hi(m):
                act.wait_ge(xt_done, m + 1)
                settle(act)
                a.activation(xt[:, ds((m % 2) * 2 * D, D)], xt_ps, ACT.Copy).then_inc(xt_hi_done, 1)

            for q in range(PIECES):
                split_hi(q, w_hi)
                if q == 0:
                    sqrt_var(1)
                if q == 1:
                    act.wait_ge(xn_done, 1)
                    a.activation(xs[:, 0:D], xn, ACT.Copy).then_inc(xs_hi_done, 1)
                if q == 4:
                    xt_hi(0)
            sqrt_var(2)
            count_hi(0)
            xs_hi(1)
            with act.Fori(1, NT - 1) as m:
                count_hi(m)
                sqrt_var(m + 2)
                xt_hi(m)
                xs_hi(m + 1)
            count_hi(NT - 1)
            xt_hi(NT - 1)

            act.wait_ge(deg_summed, 1)
            a.activation(deg_s[:], deg_f[:], ACT.Sqrt).then_inc(deg_sqrt, 1)
            act.wait_ge(spare_in, 1 + 16 * 3 * CT)
            act.wait_ge(count_done, NT)
            act.wait_ge(dis_done, 1)

            def hs_hi(m):
                a.activation(hs[:, ds(m * 2 * D, D)], t[:, ds(m * D, D)], ACT.Copy,
                             scale=dis[:, ds(m, 1)]).then_inc(hs_hi_done, 1)

            act.wait_ge(lin_read, NT - 2)
            for m in range(NT - 2):
                hs_hi(m)
            act.wait_ge(lin_read, NT - 1)
            hs_hi(NT - 2)
            act.wait_ge(lin_read, NT)
            hs_hi(NT - 1)

            act.wait_ge(consts_in, 16 * 5)
            a.activation(rw_hi[:], rw[:], ACT.Copy, scale=WSCALE).then_inc(rw_hi_done, 1)
            for r in range(NT + 1):
                if r >= 1:
                    act.wait_ge(x2t_done, r)
                    act.wait_ge(router_done, r - 1)
                    a.activation(x2t[:, 0:D], x2t_ps, ACT.Copy).then_inc(x2t_hi_done, 1)
                if r < NT:
                    sqrt_var(NT + r + 1)
                    act.wait_ge(xn_done, NT + r + 1)
                    act.wait_ge(x2t_done, r)
                    stored(act, r)
                    a.activation(xs[:, 0:D], xn, ACT.Copy).then_inc(xs_hi_done, 1)
                if 2 <= r < NT:
                    split_hi(PIECES + r - 2, e_hi[0])

            def first_turned(j):
                act.wait_ge(first_done, j + 1)
                a.activation(x4[:, j * 2 * CH:j * 2 * CH + FIRST_CH], x4_ps[j % 2][:, 0:FIRST_CH], ACT.Copy
                             ).then_inc(first_hi_done, 1)

            act.wait_ge(agg_done, 2 * NT)
            first_turned(0)
            first_turned(1)
            act.wait_ge(gap_done, 1)
            a.activation(gap_e[:], gap[:], ACT.Exp).then_inc(gap_exp, 1)
            a.activation(hold[:, 1:2], hold[:, 0:1], ACT.Gelu)

            act.dma_start(b2_row[0], b2[0:1, :].rearrange("o d -> (o d)").partition_broadcast(P)).then_inc(b2_in[0], 16)
            act.sem_inc(gelu_done, FK)

            def turned(c, j, at=0):
                act.wait_ge(x4_done, c * DK + (j + 1))
                a.activation(x4[:, j * 2 * CH + at:(2 * j + 1) * CH], x4_ps[j % 2][:, at:], ACT.Copy
                             ).then_inc(x4_hi_done, 1)

            def piece_hi(e, j, split):
                s = j % STAGES
                act.wait_ge(stage_in[s], (e + 2) * (16 * PIECES // STAGES) + 16 * (j // STAGES + 1))
                a.activation(split[:, j * D:(j + 1) * D], stage[:, s * D:(s + 1) * D], ACT.Copy,
                             scale=WSCALE).then_inc(w_hi_done, 1)

            for j in range(2, DK):
                first_turned(j)
                if j - 2 < EARLY:
                    piece_hi(0, j - 2, e_hi[1])
            act.wait_ge(ranges2_done, 1)
            more_first = act.value_load(ranges2[0:1, 3, 0:1], min_val=0, max_val=1)
            end_first = act.value_load(ranges2[0:1, 1, 0:1], min_val=1, max_val=MAXC - 2)
            for j in range(DK):
                turned(0, j, FIRST_CH)

            def chunk(c, e, split, first=False, last=False):
                if split is not None and not first:
                    for j in range(EARLY):
                        piece_hi(e, j, split)
                for f in range(FK):
                    act.wait_ge(up_done, c * FK + (f + 1))
                    settle(act)
                    a.activation(y32[:, f * CH:(f + 1) * CH], up_ps[f], ACT.Gelu, bias=b1t[:, ds(e * FK + f, 1)],
                                 scale=1.0 / WSCALE).then_inc(gelu_done, 1)
                if last:
                    return
                for j in range(DK):
                    turned(c + 1, j)
                    if split is not None and 2 <= j < 2 + PIECES - EARLY:
                        piece_hi(e, EARLY + j - 2, split)

            def next_bias(e, h, c0):
                act.wait_ge(y_ready_b2, c0 + 1)
                act.dma_start(b2_row[1 - h], b2[ds(e + 1, 1), :].rearrange("o d -> (o d)").partition_broadcast(P)
                              ).then_inc(b2_in[1 - h], 16)

            def expert(e, h, split):
                plan = act.value_load(plans[0:1, ds(e, 1)], min_val=0, max_val=PLAN ** 2 * 4 - 1)
                c0, c1 = plan // (4 * PLAN), plan // 4 % PLAN
                act.wait_ge(down_done, c0 * (2 * CT) + 1)
                if isinstance(e, int) and e == NE - 1:
                    settle(act)
                    c_last = act.value_load(last_chunk[:], min_val=NE - 1, max_val=MAXC - 3)
                    with act.If(c_last > c0):
                        with act.Fori(c0, c_last) as c:
                            chunk(c, e, None)
                    chunk(c_last, e, None, last=True)
                else:
                    next_bias(e, h, c0)
                    chunk(c0, e, split)
                    with act.If(c1 > c0 + 1):
                        with act.Fori(c0 + 1, c1) as c:
                            chunk(c, e, None)

            next_bias(0, 0, 0)
            chunk(0, 0, e_hi[1], True)
            with act.If(more_first):
                with act.Fori(1, end_first) as c:
                    chunk(c, 0, None)
            act.wait_ge(plans_done, 1)
            expert(1, 1, e_hi[0])
            with act.Fori(1, NE // 2 - 1) as pair:
                for h in range(2):
                    expert(pair * 2 + h, h, e_hi[1 - h])
            expert(NE - 2, 0, e_hi[1])
            expert(NE - 1, 1, None)

            st5 = Steps(act, act_step5)
            junk = [gx[i][:, 0:D] for i in range(2)]

            def sums_of(n):
                for r in ACT_TILES[n]:
                    act.wait_ge(fin_in[r], 16)
                    st5.link(a.activation(junk[0], fin[r], ACT.Copy, accum_out=sum5[:, r:r + 1]))
                    st5.link(a.activation(minus5[:, r:r + 1], sum5[:, r:r + 1], ACT.Copy, scale=-1.0 / D))
                    st5.did(a.activation(junk[1], fin[r], ACT.Square, bias=minus5[:, r:r + 1],
                                         accum_out=square5[:, r:r + 1]))
                st5.wait()
                cs = slice(ACT_TILES[n][0], ACT_TILES[n][-1] + 1)
                a.activation(square5[:, cs], square5[:, cs], ACT.Copy, scale=1.0 / D).then_inc(square5_done, 1)

            sums_of(0)
            for n, tiles in enumerate(LAST_GROUPS):
                cs = slice(tiles[0], tiles[-1] + 1)
                act.wait_ge(var5_done, n + 1)
                a.activation(std5[:, cs], var5[:, cs], ACT.Sqrt).then_inc(std5_done, 1)
                if n + 1 < len(ACT_TILES):
                    sums_of(n + 1)
                act.wait_ge(rstd5_done, n + 1)
                for r in tiles:
                    act.wait_ge(weighed, r + 1)
                    a.activation(fin[r], fin[r], ACT.Copy, scale=rstd5[:, r:r + 1]).then_inc(scaled, 1)

        @block.vector
        def _(dve):
            v = nc.vector
            step = Steps(dve, dve_step)

            def newton(r, x, q, steps):
                steps.link(v.tensor_tensor(q, r, x, ALU.mult))
                steps.link(v.tensor_tensor(q, q, r, ALU.mult))
                steps.link(v.tensor_scalar(q, q, -0.5, 1.5, ALU.mult, ALU.add))
                return v.tensor_tensor(r, r, q, ALU.mult)

            def carry_wait(col):
                v.tensor_copy(hold[:, 0:1], col)

            def layernorm_stats(xm, eps, steps):
                steps.did(v.bn_stats(stats[:, 0:6], xm[0]))
                steps.did(v.bn_stats(stats[:, 6:12], xm[1]))
                steps.wait()
                carry_wait(stats[:, 0:1])
                steps.link(v.bn_aggr(mv[:], stats[:]))
                return v.tensor_scalar(std[:, 0:1], mv[:, 1:2], eps, None, ALU.add)

            def layernorm_a(m):
                xm = t[:, ds(m * D, HALF)], t[:, ds(m * D + HALF, HALF)]
                layernorm_stats(xm, EPS1, step).then_inc(var_done, 1)

            def layernorm_b(m):
                dve.wait_ge(std_done, m + 1)
                step.link(v.reciprocal(rstd[:], std[:, 1:2]))
                step.link(newton(rstd[:], std[:, 0:1], q_col[:], step))
                dve.wait_ge(xs_done, m)
                v.tensor_scalar(xn, t[:, ds(m * D, D)], mv[:, 0:1], rstd[:],
                                ALU.subtract, ALU.mult).then_inc(xn_done, 1)

            v.memset(ident[:], 0.0).then_inc(blank, 1)
            v.memset(tri[:], 1.0).then_inc(blank, 1)
            v.memset(ident16[:], 0.0).then_inc(blank, 1)
            v.memset(zeros16[:], 0.0).then_inc(blank, 1)
            v.memset(tri16[:], 1.0).then_inc(blank, 1)
            step.did(v.memset(first_v[:], 0.0))
            step.did(v.memset(last_v[:], 0.0))
            dve.wait_ge(dst_rows_in, 32)
            dve.wait_ge(consts_done, RANGE_CONSTS)
            step.did(v.tensor_scalar(tile_from[:], tile_no[:], -1.0, BIG, ALU.mult, ALU.add))
            step.did(v.tensor_scalar(tile_to[:], tile_no[:], 1.0, None, ALU.add))
            halves = ((0, P), (1, ET - P))
            for h, n in halves:
                step.did(v.tensor_copy(dst_rf[0:n, h, :], dst_r[0:n, h, :]))
            step.wait()
            for h, n in halves:
                step.did(v.tensor_reduce(tile_min[0:n, h:h + 1], dst_rf[0:n, h, :], AXX, ALU.min))
                step.did(v.tensor_reduce(tile_max[0:n, h:h + 1], dst_rf[0:n, h, :], AXX, ALU.max))
            step.wait()
            for h, n in halves:
                step.did(v.tensor_scalar(overlap[0:n, h, 0:NT], block_lo[0:n, :], tile_max[0:n, h:h + 1], None, ALU.is_le))
            step.wait()
            for h, n in halves:
                ov = overlap[0:n, h, 0:NT]
                step.did(v.scalar_tensor_tensor(ov, block_hi[0:n, :], tile_min[0:n, h:h + 1], ov, ALU.is_gt, ALU.mult))
            step.wait()
            for h, n in halves:
                ov = overlap[0:n, h, 0:NT]
                step.did(v.tensor_scalar(first_v[0:n, h, 0:NT], ov, tile_from[0:n, h:h + 1], None, ALU.mult))
                step.did(v.tensor_scalar(last_v[0:n, h, 0:NT], ov, tile_to[0:n, h:h + 1], None, ALU.mult))
            step.wait()
            v.engine_nop().then_inc(spans_cols, 1)
            dve.wait_ge(x0_in, 16)
            layernorm_a(0)
            dve.wait_ge(spans_tr, 1)
            step.did(v.tensor_reduce(span[0:NT, 0:1], misc_ps[0:NT, 0:2 * P], AXX, ALU.max))
            step.link(v.tensor_reduce(span[0:NT, 1:2], misc_ps[0:NT, 2 * P:4 * P], AXX, ALU.max))
            step.link(v.tensor_scalar(span[0:NT, 2:3], span[0:NT, 0:1], -1.0, BIG, ALU.mult, ALU.add))
            step.did(v.tensor_scalar(span[0:NT, 3:4], span[0:NT, 2:3], ET - 1.0, None, ALU.min))
            step.link(v.tensor_tensor(span[0:NT, 4:5], span[0:NT, 1:2], span[0:NT, 2:3], ALU.subtract))
            step.link(v.tensor_scalar(span[0:NT, 4:5], span[0:NT, 4:5], 1.0, None, ALU.max))
            step.link(v.tensor_scalar(steps_in[0:NT, :], step_from[0:NT, :], span[0:NT, 4:5], None, ALU.is_lt))
            v.tensor_reduce(span[0:NT, 5:6], steps_in[0:NT, :], AXX, ALU.add).then_inc(spans_n, 1)
            dve.wait_ge(edges_in, 32)
            step.did(v.memset(src_f[:, ET:], -1.0))
            step.did(v.memset(dst_f[:, ET:], -1.0))
            step.did(v.tensor_copy(src_f[:, 0:ET], src_i[:]))
            step.did(v.tensor_copy(dst_f[:, 0:ET], dst_i[:]))
            layernorm_b(0)
            dve.wait_ge(spans_ps, 1)
            step.link(v.tensor_copy(span_row[0:1, 0:48], misc_ps[0:1, 0:48]))
            step.did(v.tensor_copy(ranges[0:1, 0, 0:NT], span_row[0:1, 32:32 + NT]))
            step.did(v.scalar_tensor_tensor(steps_f[0:1, :], span_row[0:1, 0:NT], SPLIT + 1.0, span_row[0:1, 16:16 + NT],
                                            ALU.mult, ALU.add))
            step.wait()
            v.tensor_copy(ranges[0:1, 1, 0:NT], steps_f[0:1, :]).then_inc(ranges_done, 1)
            dve.wait_ge(ranges_done, 1)
            step.wait()

            def onehot_pair(m, k, u, n, w=N):
                dve.wait_ge(onehot_used, n + 1)
                v.tensor_scalar(onehots[:, u * OHW:u * OHW + w], iota16[:, 0:w], src_f[:, ds(k, 1)], None, ALU.is_equal)
                v.tensor_scalar(onehots[:, u * OHW + NP:(u + 1) * OHW], iota16[:, ds(m * P, P)], dst_f[:, ds(k, 1)],
                                None, ALU.is_equal).then_inc(onehot_done, 1)

            def edge_onehots(m):
                first = dve.value_load(ranges[0:1, 0, ds(m, 1)], min_val=0, max_val=ET - 1)
                steps = dve.value_load(ranges[0:1, 1, ds(m, 1)], min_val=0, max_val=SPLIT ** 2 - 1)
                s0, s1 = steps // SPLIT, steps % SPLIT
                for u in range(MAIN):
                    onehot_pair(m, first + u, u % RING, m * MAIN + s0 * EXTRA + u, N if u else NP)
                with dve.If(s1 > s0):
                    with dve.Fori(s0, s1) as i:
                        k = dve.snap(first + MAIN + (i - s0) * EXTRA).with_bounds(min_val=0, max_val=ETP - EXTRA)
                        for u in range(EXTRA):
                            onehot_pair(m, k + u, RING + u, m * MAIN + i * EXTRA + (MAIN + u + RING - 1 - EXTRA))

            def count_lo(m):
                dve.wait_ge(count_hi_read, m + 1)
                dve.wait_ge(count_lo_done, m)
                v.tensor_tensor(ct_lo_16[:], count_ps, ct_hi[:, ds(m * NP, NP)], ALU.subtract).then_inc(count_lo_read, 1)

            def xt_lo(m):
                dve.wait_ge(xt_hi_done, m + 1)
                v.tensor_tensor(xt[:, ds((m % 2) * 2 * D + D, D)], xt_ps, xt[:, ds((m % 2) * 2 * D, D)],
                                ALU.subtract).then_inc(xt_lo_done, 1)

            def h_copy(m, lin_ps=lin_ps):
                dve.wait_ge(lin_done, m + 1)
                for n in range(2):
                    ins = v.scalar_tensor_tensor(t[:, ds(m * D + n * HALF, HALF)], lin_ps[:, n * HALF:(n + 1) * HALF],
                                                 1.0 / WSCALE, b_row[:, n * HALF:(n + 1) * HALF], ALU.mult, ALU.add)
                ins.then_inc(lin_read, 1)

            dve.wait_ge(consts_done, EDGE_CONSTS)
            dve.sem_inc(onehot_used, RING - 1)
            edge_onehots(0)
            dve.wait_ge(x1_in, 16)
            layernorm_a(1)
            xt_lo(0)
            count_lo(0)
            layernorm_b(1)
            edge_onehots(1)
            dve.wait_ge(b_in, 16)
            dve.wait_ge(xrest_in, 16)
            base = step.k
            LINKS1 = 8
            with dve.Fori(1, NT - 1) as m:
                step.enter((m - 1) * LINKS1 + base)
                layernorm_a(m + 1)
                count_lo(m)
                layernorm_b(m + 1)
                xt_lo(m)
                edge_onehots(m + 1)
                h_copy(m - 1)
                assert step.k == LINKS1
            step.enter((NT - 2) * LINKS1 + base)
            count_lo(NT - 1)
            xt_lo(NT - 1)

            dve.wait_ge(deg_hi_done, 1)
            step.link(v.tensor_copy(deg_f[:], misc_ps[:, 0:NT]))
            v.tensor_scalar(over[:], misc_ps[:, 0:NT], EXACT16, None, ALU.is_ge).then_inc(over_cols, 1)
            dve.wait_ge(over_ps, 1)
            step.link(v.tensor_reduce(over_row[0:1, 0:1], misc_ps[0:1, 16:16 + NT], AXX, ALU.max))
            v.tensor_copy(over_i[0:1, 0:1], over_row[0:1, 0:1]).then_inc(over_done, 1)
            dve.wait_ge(deg_done, 1)
            v.tensor_tensor(deg_f[:], deg_f[:], deg_lo_ps, ALU.add).then_inc(deg_summed, 1)
            dve.wait_ge(deg_sqrt, 1)
            step.link(v.reciprocal(dis[:], deg_s[:]))
            newton(dis[:], deg_f[:], q_dis[:], step).then_inc(dis_done, 1)
            dve.wait_ge(dis_done, 1)

            def hs_lo(m):
                dve.wait_ge(hs_hi_done, m + 1)
                v.scalar_tensor_tensor(hs[:, ds(m * 2 * D + D, D)], t[:, ds(m * D, D)], dis[:, ds(m, 1)],
                                       hs[:, ds(m * 2 * D, D)], ALU.mult, ALU.subtract).then_inc(hs_lo_done, 1)

            h_copy(NT - 2)
            hs_lo(0)
            for m in range(1, NT - 2):
                hs_lo(m)
            h_copy(NT - 1, xt_ps)
            hs_lo(NT - 2)
            hs_lo(NT - 1)

            st3 = Steps(dve, dve_step3)
            dve.wait_ge(consts_in, 16 * 5)
            dve.wait_ge(rw_hi_done, 1)
            v.scalar_tensor_tensor(rw_lo[:], rw[:], WSCALE, rw_hi[:], ALU.mult, ALU.subtract).then_inc(rw_lo_done, 1)
            st3.link(v.tensor_scalar(first_slot[:], first_slot[:], float(P), None, ALU.mult))
            st3.link(v.tensor_copy(carry[:], first_slot[:]))

            def x2t_lo(r):
                dve.wait_ge(x2t_hi_done, r + 1)
                v.tensor_tensor(x2t[:, D:], x2t_ps, x2t[:, 0:D], ALU.subtract).then_inc(x2t_lo_done, 1)

            def add_agg(r):
                dve.wait_ge(x_again0, 16)
                if r >= 2:
                    dve.wait_ge(x_again1, 16)
                for n in range(2):
                    cs = slice(r * D + n * HALF, r * D + (n + 1) * HALF)
                    dve.wait_ge(agg_done, 2 * r + n + 1)
                    st3.did(v.scalar_tensor_tensor(t[:, cs], agg_ps[r % 2][:, n * HALF:(n + 1) * HALF], dis[:, r:r + 1],
                                                   t[:, cs], ALU.mult, ALU.add))
                st3.wait()
                layernorm_stats((t[:, r * D:r * D + HALF], t[:, r * D + HALF:(r + 1) * D]), EPS1, st3
                                ).then_inc(var_done, 1)
                if 1 <= r < NT - 1:
                    x2t_lo(r - 1)
                dve.wait_ge(std_done, NT + r + 1)
                st3.link(v.reciprocal(rstd[:], std[:, 1:2]))
                st3.link(newton(rstd[:], std[:, 0:1], q_col[:], st3))
                dve.wait_ge(xs_done, NT + r)
                stored(dve, r)
                v.tensor_scalar(xn, t[:, r * D:(r + 1) * D], mv[:, 0:1], rstd[:], ALU.subtract,
                                ALU.mult).then_inc(xn_done, 1)
                if r == NT - 1:
                    x2t_lo(r - 1)
                    dve.wait_ge(xs_hi_done, NT + r + 1)
                    v.tensor_tensor(xs[:, D:], xn, xs[:, 0:D], ALU.subtract).then_inc(xs_done, 1)

            def choose(r):
                dve.wait_ge(router_done, r + 1)
                st3.link(v.scalar_tensor_tensor(logits[:], router_ps[:, 0:NE], 1.0 / WSCALE, rb_row[:], ALU.mult, ALU.add))
                st3.link(v.max(top[:], logits[:]))
                st3.did(v.tensor_tensor(gap[:, r:r + 1], top[:, 1:2], top[:, 0:1], ALU.subtract))
                st3.link(v.max_index(top_i[:], top[:], logits[:]))
                st3.link(v.tensor_copy(top_f[:], top_i[:, 0:2]))
                for n in range(2):
                    st3.did(v.tensor_scalar(oh[:, n * NE:(n + 1) * NE], expert_no[:], top_f[:, n:n + 1], None,
                                            ALU.is_equal))
                st3.wait()
                v.tensor_tensor(mask[:], oh[:, 0:NE], oh[:, NE:2 * NE], ALU.add).then_inc(mask_done, 1)
                st3.did(v.tensor_copy(oh_all[:, r * 2 * NE:(r + 1) * 2 * NE], oh[:]))

            def place(r):
                dve.wait_ge(rank_done, r + 1)
                st3.link(v.tensor_tensor(slot_of[:], rank_ps[:, 0:NE], carry[:], ALU.add))
                st3.link(v.tensor_tensor(slot_pick[:].rearrange("p (n e) -> p n e", n=2),
                                         oh[:].rearrange("p (n e) -> p n e", n=2),
                                         slot_of[:].unsqueeze(1).to_broadcast([P, 2, NE]), ALU.mult))
                st3.link(v.tensor_reduce(slot_f[:], slot_pick[:].rearrange("p (n e) -> p n e", n=2), AXX, ALU.add))
                st3.did(v.tensor_scalar(slot_m[:], slot_f[:], float(CPT), None, ALU.mult))
                st3.link(v.tensor_copy(slot_i[:], slot_f[:]))
                st3.link(v.tensor_scalar(slot_i[:], slot_i[:], 7, None, ALU.logical_shift_right))
                v.scalar_tensor_tensor(slots[:, 2 * r:2 * r + 2], slot_i[:], -float(P * CPT - 1), slot_m[:],
                                       ALU.mult, ALU.add).then_inc(slots_done, 1)
                if r == NT - 1:
                    st3.link(v.tensor_tensor(cnt[:], rank_ps[0:1, 2 * NE:3 * NE], carry[0:1, :], ALU.add))
                    st3.link(v.tensor_tensor(cnt[:], cnt[:], first_slot[0:1, :], ALU.subtract))
                    st3.did(v.tensor_copy(last_ends[:, r:r + 1], cnt[0:1, NE - 1:NE]))
                else:
                    st3.link(v.tensor_tensor(carry[:], rank_ps[:, NE:2 * NE], carry[:], ALU.add))
                    if r == FIRST_TILES - 1:
                        st3.link(v.tensor_scalar(carry[:, 0:1], carry[:, 0:1], float(FIRST_CH), None, ALU.max))
                    st3.did(v.tensor_tensor(last_ends[:, r:r + 1], carry[0:1, NE - 1:NE], first_slot[0:1, NE - 1:NE],
                                            ALU.subtract))

            def first_turned(j):
                dve.wait_ge(first_hi_done, j + 1)
                v.tensor_tensor(x4[:, (2 * j + 1) * CH:(2 * j + 1) * CH + FIRST_CH], x4_ps[j % 2][:, 0:FIRST_CH],
                                x4[:, j * 2 * CH:j * 2 * CH + FIRST_CH], ALU.subtract).then_inc(first_lo_done, 1)

            for r in range(NT + 2):
                if 2 <= r:
                    choose(r - 2)
                if r == NT + 1:
                    first_turned(0)
                if r < NT:
                    add_agg(r)
                if r == NT:
                    x2t_lo(r - 1)
                if r == NT + 1:
                    st3.wait()
                    v.engine_nop().then_inc(gap_done, 1)
                if 2 <= r:
                    place(r - 2)
            dve.wait_ge(gap_exp, 1)
            st3.link(v.tensor_scalar(wt[:, NT:], gap_e[:], 1.0, None, ALU.add))
            st3.link(v.reciprocal(wt[:, 0:NT], wt[:, NT:]))
            st3.link(v.tensor_tensor(wt[:, NT:], gap_e[:], wt[:, 0:NT], ALU.mult))
            oh_v = oh_all[:].rearrange("p (r n e) -> p n r e", n=2, e=NE)
            for n, d in ((0, cw), (1, cw2)):
                st3.did(v.tensor_tensor(d[:].rearrange("p (r e) -> p r e", e=NE), oh_v[:, n],
                                        wt[:, n * NT:(n + 1) * NT].unsqueeze(2).to_broadcast([P, NT, NE]), ALU.mult))
            st3.wait()
            v.tensor_tensor(cw[:], cw[:], cw2[:], ALU.add).then_inc(cw_done, 1)
            first_turned(1)
            st3.did(v.memset(scan[:], 0.0))
            st3.link(v.tensor_scalar(ranges2_f[:, 0, :], cnt[:], float(CH), 1.0, ALU.is_gt, ALU.add))
            for k in range(2, CPE):
                st3.link(v.scalar_tensor_tensor(ranges2_f[:, 0, :], cnt[:], float(k * CH), ranges2_f[:, 0, :],
                                                ALU.is_gt, ALU.add))
            st3.link(v.tensor_copy(scan[:, 0, NE:], ranges2_f[:, 0, :]))
            for k in range(3):
                st3.link(v.tensor_tensor(scan[:, k + 1, NE:], scan[:, k, NE:], scan[:, k, NE - 2 ** k:2 * NE - 2 ** k],
                                         ALU.add))
            st3.did(v.tensor_copy(ranges2_f[:, 1, :], scan[:, 3, NE:]))
            st3.did(v.tensor_scalar(ranges2_f[:, 3, :], ranges2_f[:, 0, :], 1.0, 1.0, ALU.subtract, ALU.min))
            st3.did(v.tensor_scalar(ranges2_f[:, 2, :], ranges2_f[:, 0, :], -1.0, float(CPE), ALU.mult, ALU.add))
            st3.link(v.tensor_tensor(scan[:, 0, 0:NE], scan[:, 3, NE:], ranges2_f[:, 0, :], ALU.subtract))
            st3.link(v.tensor_copy(ranges2_f[:, 0, :], scan[:, 0, 0:NE]))
            v.tensor_copy(ranges2[:], ranges2_f[:]).then_inc(ranges2_done, 1)
            st3.link(v.tensor_scalar(last_chunk[:], ranges2_f[:, 1, NE - 1:NE], -1.0, None, ALU.add))
            first_turned(2)
            over_e = [1, MAXC, NE]
            st3.link(v.tensor_tensor(chunk_skip[:], chunk_i[:].unsqueeze(2).to_broadcast(over_e),
                                     ranges2_f[:, 1, :].unsqueeze(1).to_broadcast(over_e), ALU.is_ge))
            st3.link(v.tensor_tensor(chunk_skip[:], chunk_skip[:],
                                     ranges2_f[:, 2, :].unsqueeze(1).to_broadcast(over_e), ALU.mult))
            st3.link(v.tensor_reduce(chunk_f[:], chunk_skip[:], AXX, ALU.add))
            st3.link(v.tensor_tensor(chunk_f[:], chunk_f[:], chunk_i[:], ALU.add))
            v.tensor_scalar(chunk_at[:], chunk_f[:], float(NE * CPE - 1), None, ALU.min).then_inc(chunks_done, 1)
            first_turned(3)
            dve.wait_ge(ranges2_done, 1)
            more_first = dve.value_load(ranges2[0:1, 3, 0:1], min_val=0, max_val=1)
            end_first = dve.value_load(ranges2[0:1, 1, 0:1], min_val=1, max_val=MAXC - 2)
            st4 = Steps(dve, dve_step4)
            LINKS4 = FK
            dve.sem_inc(x4_lo_done, 2)
            dve.sem_inc(down_read, 2)
            dve.sem_inc(y_ready_b2, 1)
            dve.sem_inc(rows_added, 1)

            def turned(c, j, at=0):
                dve.wait_ge(x4_hi_done, c * DK + (j + 1))
                v.tensor_tensor(x4[:, (2 * j + 1) * CH + at:(j + 1) * 2 * CH], x4_ps[j % 2][:, at:],
                                x4[:, j * 2 * CH + at:(2 * j + 1) * CH], ALU.subtract).then_inc(x4_lo_done, 1)

            def weights_of(c):
                dve.wait_ge(cw_in, c * (16 * CT) + 16 * CT)
                v.tensor_copy(cw_chunk[:], cw_next[:]).then_inc(cw_copied, 1)

            def piece_lo(e, j, split):
                hi, lo = split
                s = j % STAGES
                dve.wait_ge(w_hi_done, e * PIECES + (2 * PIECES + j + 1))
                v.scalar_tensor_tensor(lo[:, j * D:(j + 1) * D], stage[:, s * D:(s + 1) * D], WSCALE,
                                       hi[:, j * D:(j + 1) * D], ALU.mult, ALU.subtract).then_inc(e_lo_done, 1)

            for j in range(DK - EARLY, DK):
                first_turned(j)
                piece_lo(0, j - (DK - EARLY), (e_hi[1], e_lo[1]))
            for j in range(DK):
                turned(0, j, FIRST_CH)
            weights_of(0)
            st3.link(v.tensor_scalar(plans_f[:], ranges2_f[:, 0, :], float(PLAN), None, ALU.mult))
            st3.link(v.tensor_tensor(plans_f[:], plans_f[:], ranges2_f[:, 1, :], ALU.add))
            st3.link(v.tensor_scalar(plans_f[:], plans_f[:], 4.0, None, ALU.mult))
            for wide in WIDTHS[:-1]:
                st3.link(v.scalar_tensor_tensor(plans_f[:], cnt[:], float(wide), plans_f[:], ALU.is_gt, ALU.add))
            v.tensor_copy(plans[:], plans_f[:]).then_inc(plans_done, 1)

            def chunk(c, e, h, split, first=False, last=False):
                st4.enter(c * LINKS4)
                if split is not None and not first:
                    for j in range(EARLY):
                        piece_lo(e, j, split)
                for f in range(FK):
                    fs = slice(f * CH, (f + 1) * CH)
                    dve.wait_ge(gelu_done, c * FK + (FK + f + 1))
                    st4.link(v.tensor_copy(y_hi[:, fs], y32[:, fs]))
                    v.tensor_tensor(y_lo[:, fs], y32[:, fs], y_hi[:, fs], ALU.subtract).then_inc(y_lo_done, 1)
                dve.wait_ge(cw_copied, c + 1)
                dve.wait_ge(rows_added, c + 1)
                if not last:
                    turned(c + 1, 0)
                    turned(c + 1, 1)
                for i in range(CT):
                    for n in range(2):
                        k = 2 * i + n
                        o = y_out[i][:, n * HALF:(n + 1) * HALF]
                        dve.wait_ge(down_done, c * (2 * CT) + (k + 2))
                        ins = v.scalar_tensor_tensor(o, down_ps[n], 1.0 / WSCALE, b2_row[h][:, n * HALF:(n + 1) * HALF],
                                                     ALU.mult, ALU.add)
                        ins.then_inc(down_read, 1)
                        dve.wait_ge(down_read, c * (2 * CT) + (k + 3))
                        ins = v.tensor_scalar(o, o, cw_chunk[:, ds(i * NE + e, 1)], None, ALU.mult)
                        if n:
                            ins.then_inc(y_ready, 1)
                        if not last:
                            turned(c + 1, k + 2)
                        if split is not None and 1 <= k <= PIECES - EARLY:
                            piece_lo(e, EARLY + k - 1, split)
                if last:
                    return
                dve.wait_ge(y_ready, c * CT + CT)
                v.tensor_copy(hold[:, 1:2], hold[:, 0:1]).then_inc(y_ready_b2, 1)
                weights_of(c + 1)

            def expert(e, h, pair, split):
                plan = dve.value_load(plans[0:1, ds(e, 1)], min_val=0, max_val=PLAN ** 2 * 4 - 1)
                c0, c1 = plan // (4 * PLAN), plan // 4 % PLAN
                dve.wait_ge(b2_in[h], pair * 16 + 16)
                if isinstance(e, int) and e == NE - 1:
                    settle(dve)
                    c_last = dve.value_load(last_chunk[:], min_val=NE - 1, max_val=MAXC - 3)
                    with dve.If(c_last > c0):
                        with dve.Fori(c0, c_last) as c:
                            chunk(c, e, h, None)
                    chunk(c_last, e, h, None, last=True)
                else:
                    chunk(c0, e, h, split)
                    with dve.If(c1 > c0 + 1):
                        with dve.Fori(c0 + 1, c1) as c:
                            chunk(c, e, h, None)

            dve.wait_ge(b2_in[0], 16)
            chunk(0, 0, 0, (e_hi[1], e_lo[1]), True)
            st3.link(v.tensor_tensor(last_base[:], ranges2_f[:, 1, NE - 1:NE], ranges2_f[:, 0, NE - 1:NE], ALU.subtract))
            st3.link(v.tensor_scalar(last_base[:], last_base[:], float(CH), -float(CH), ALU.mult, ALU.add))
            st3.link(v.tensor_scalar(last_ends[:], last_ends[:], last_base[:, 0:1], None, ALU.subtract))
            st3.link(v.tensor_scalar(needs_f[:], last_ends[:], 0.0, 1.0, ALU.is_gt, ALU.add))
            for i in range(1, CT):
                st3.link(v.scalar_tensor_tensor(needs_f[:], last_ends[:], float(i * P), needs_f[:], ALU.is_gt, ALU.add))
            v.tensor_copy(needs[:], needs_f[:]).then_inc(needs_done, 1)
            with dve.If(more_first):
                with dve.Fori(1, end_first) as c:
                    chunk(c, 0, 0, None)
            expert(1, 1, 0, (e_hi[0], e_lo[0]))
            with dve.Fori(1, NE // 2 - 1) as pair:
                for h in range(2):
                    expert(pair * 2 + h, h, pair, (e_hi[1 - h], e_lo[1 - h]))
            expert(NE - 2, 0, NE // 2 - 1, (e_hi[1], e_lo[1]))
            expert(NE - 1, 1, NE // 2 - 1, None)

            st5 = Steps(dve, dve_step5)

            def weigh(r):
                by_act = any(r in pair for pair in ACT_TILES)
                mean, centre = (minus5[:, r:r + 1], ALU.add) if by_act else (mv5[:, r, 0:1], ALU.subtract)
                v.scalar_tensor_tensor(fin[r], fin[r], mean, lnw_row[:], centre, ALU.mult).then_inc(weighed, 1)

            for n, tiles in enumerate(LAST_GROUPS):
                own = tiles
                if n < len(ACT_TILES):
                    own = tiles[len(ACT_TILES[n]):]
                cs = slice(own[0], own[-1] + 1)
                for r in own:
                    dve.wait_ge(fin_in[r], 16)
                    st5.did(v.bn_stats(stats5[:, r, 0:6], fin[r][:, 0:HALF]))
                    st5.did(v.bn_stats(stats5[:, r, 6:12], fin[r][:, HALF:D]))
                st5.wait()
                for r in own:
                    st5.did(v.bn_aggr(mv5[:, r, :], stats5[:, r, :]))
                st5.wait()
                ins = v.tensor_scalar(var5[:, cs], mv5[:, cs, 1], EPS2, None, ALU.add)
                if n < len(ACT_TILES):
                    st5.did(ins)
                    cs = slice(tiles[0], own[0])
                    dve.wait_ge(square5_done, n + 1)
                    ins = v.tensor_scalar(var5[:, cs], square5[:, cs], EPS2, None, ALU.add)
                    st5.wait()
                ins.then_inc(var5_done, 1)
                cs = slice(tiles[0], tiles[-1] + 1)
                for r in tiles[:-1]:
                    weigh(r)
                dve.wait_ge(std5_done, n + 1)
                dve.wait_ge(var5_done, n + 1)
                st5.link(v.reciprocal(rstd5[:, cs], std5[:, cs]))
                newton(rstd5[:, cs], var5[:, cs], q5[:, cs], st5).then_inc(rstd5_done, 1)
                weigh(tiles[-1])

        @block.tensor
        def _(pe):
            mm = nc.tensor.matmul
            pe.wait_ge(consts_done, PE_CONSTS)
            pe.wait_ge(spans_cols, 1)
            for i, vv in enumerate((first_v, last_v)):
                for h in range(2):
                    ins = nc.tensor.transpose(misc_ps[:, (2 * i + h) * P:(2 * i + h + 1) * P], vv[:, h, :], ident[:])
            ins.then_inc(spans_tr, 1)
            pe.wait_ge(spans_n, 1)
            mm(misc_ps[0:1, 0:NT], span[0:NT, 5:6], tri[0:NT, 0:NT], start=True, stop=True)
            mm(misc_ps[0:1, 16:16 + NT], span[0:NT, 5:6], ident[0:NT, 0:NT], start=True, stop=True)
            mm(misc_ps[0:1, 32:32 + NT], span[0:NT, 3:4], ident[0:NT, 0:NT], start=True,
               stop=True).then_inc(spans_ps, 1)

            def transposed(out, rows):
                for j in range(DK):
                    for h in range(2):
                        ins = mm(out[:, j * P:(j + 1) * P], rows[:, h * D + j * P:h * D + (j + 1) * P], ident16[:],
                                 start=(h == 0), stop=(h == 1), skip_group_check=True)
                return ins

            def turn(m):
                pe.wait_ge(xs_done, m + 1)
                pe.wait_ge(xt_lo_done, m)
                transposed(xt_ps, xs).then_inc(xt_done, 1)

            def count_pair(m, u, n, start):
                pe.wait_ge(onehot_done, n + 1)
                for lo in range(0, N, HALF):
                    w = min(HALF, (NP if start else N) - lo)
                    ins = mm(count_ps[:, lo:lo + w], onehots[:, u * OHW + NP:(u + 1) * OHW],
                             onehots[:, u * OHW + lo:u * OHW + lo + w], start=start, stop=False, skip_group_check=True)
                ins.then_inc(onehot_used, 1)

            def count_block(m):
                pe.wait_ge(count_lo_read, m)
                steps = pe.value_load(ranges[0:1, 1, ds(m, 1)], min_val=0, max_val=SPLIT ** 2 - 1)
                s0, s1 = steps // SPLIT, steps % SPLIT
                for u in range(MAIN):
                    count_pair(m, u % RING, m * MAIN + s0 * EXTRA + u, u == 0)
                with pe.If(s1 > s0):
                    with pe.Fori(s0, s1) as i:
                        for u in range(EXTRA):
                            count_pair(m, RING + u, m * MAIN + i * EXTRA + (MAIN + u), False)
                mm(count_ps[:, ds(m * P, P)], ident16[:], ident16[:], start=False, stop=False, skip_group_check=True)
                for lo in range(0, NP, HALF):
                    ins = mm(count_ps[:, lo:lo + 1], zeros16[:], zeros16[:, 0:1], start=False, stop=True,
                             skip_group_check=True)
                ins.then_inc(count_done, 1)

            def linear(m, parts=range(2 * DK), splitting=False, out=lin_ps):
                if parts[0] == 0:
                    pe.wait_ge(xt_lo_done, m + 1)
                    if not splitting and out is lin_ps:
                        pe.wait_ge(lin_read, m)
                for part in parts:
                    n, k = part // DK, part % DK
                    if splitting:
                        pe.wait_ge(w_lo_done, k + 1)
                    x_hi = xt[:, ds((m % 2) * 2 * D + k * P, P)]
                    x_lo = xt[:, ds((m % 2) * 2 * D + D + k * P, P)]
                    ws = slice(k * D + n * HALF, k * D + (n + 1) * HALF)
                    o = out[:, n * HALF:(n + 1) * HALF]
                    mm(o, x_hi, w_hi[:, ws], start=(k == 0), stop=False)
                    mm(o, x_hi, w_lo[:, ws], start=False, stop=False)
                    ins = mm(o, x_lo, w_hi[:, ws], start=False, stop=(k == DK - 1))
                if parts[-1] == 2 * DK - 1:
                    ins.then_inc(lin_done, 1)

            pe.wait_ge(ranges_done, 1)
            pe.wait_ge(consts_done, ALL_CONSTS)
            turn(0)
            count_block(0)
            linear(0, range(DK), True)
            count_block(1)
            turn(1)
            linear(0, range(DK, 2 * DK))
            with pe.Fori(1, NT - 2) as m:
                count_block(m + 1)
                turn(m + 1)
                linear(m)

            count_block(NT - 1)
            turn(NT - 1)

            pe.wait_ge(count_hi_read, NT)
            for r in range(NT):
                for m in range(NT):
                    cs = slice(m * NP + r * P, m * NP + (r + 1) * P)
                    ins = mm(misc_ps[:, r:r + 1], ct_hi[:, cs], ones16[:, 0:1], start=(m == 0), stop=(m == NT - 1),
                             skip_group_check=True)
                if r == NT - 1:
                    ins.then_inc(deg_hi_done, 1)
                linear(NT - 2, range(r, r + 1))
            pe.wait_ge(over_cols, 1)
            mm(misc_ps[0:1, 16:16 + NT], ones16[:, 0:1], over[:], start=True, stop=True).then_inc(over_ps, 1)
            linear(NT - 2, range(NT, NT + 3))
            pe.wait_ge(over_done, 1)
            big_counts = pe.value_load(over_i[0:1, 0:1], min_val=0, max_val=P)
            mm(deg_lo_ps, zeros16[:], zeros16[:, 0:NT], start=True, stop=False, skip_group_check=True)
            with pe.If(big_counts):
                pe.wait_ge(count_lo_done, NT)
                for r in range(NT):
                    for m in range(NT):
                        cs = slice(m * NP + r * P, m * NP + (r + 1) * P)
                        mm(deg_lo_ps[:, r:r + 1], ct_lo[:, cs], ones16[:, 0:1], start=False, stop=False,
                           skip_group_check=True)
            mm(deg_lo_ps, zeros16[:], zeros16[:, 0:NT], start=False, stop=True, skip_group_check=True).then_inc(deg_done, 1)
            linear(NT - 2, range(NT + 3, 2 * DK))
            linear(NT - 1, out=xt_ps)

            def aggregate(r, n):
                o = agg_ps[r % 2][:, n * HALF:(n + 1) * HALF]
                if r >= 2:
                    pe.wait_ge(var_done, NT + r - 1)
                for m in range(NT):
                    cs = slice(m * NP + r * P, m * NP + (r + 1) * P)
                    at = m * 2 * D + n * HALF
                    if r == 0:
                        pe.wait_ge(hs_lo_done, m + 1)
                    mm(o, ct_hi[:, cs], hs[:, at:at + HALF], start=(m == 0), stop=False, skip_group_check=True)
                    mm(o, ct_hi[:, cs], hs[:, D + at:D + at + HALF], start=False, stop=False, skip_group_check=True)
                with pe.If(big_counts):
                    for m in range(NT):
                        cs = slice(m * NP + r * P, m * NP + (r + 1) * P)
                        at = m * 2 * D + n * HALF
                        mm(o, ct_lo[:, cs], hs[:, at:at + HALF], start=False, stop=False, skip_group_check=True)
                mm(o[:, 0:P], zeros16[:], zeros16[:], start=False, stop=True, skip_group_check=True).then_inc(agg_done, 1)

            def turn2(r):
                pe.wait_ge(xs_done, NT + r + 1)
                pe.wait_ge(x2t_lo_done, r)
                transposed(x2t_ps, xs).then_inc(x2t_done, 1)

            def route(r):
                pe.wait_ge(x2t_lo_done, r + 1)
                pe.wait_ge(mask_done, r)
                if r == 0:
                    pe.wait_ge(rw_lo_done, 1)
                o = router_ps[:, 0:NE]
                for k in range(DK):
                    hi, lo, ws = slice(k * P, (k + 1) * P), slice(D + k * P, D + (k + 1) * P), slice(k * NE, (k + 1) * NE)
                    mm(o, x2t[:, hi], rw_hi[:, ws], start=(k == 0), stop=False)
                    mm(o, x2t[:, hi], rw_lo[:, ws], start=False, stop=False)
                    ins = mm(o, x2t[:, lo], rw_hi[:, ws], start=False, stop=(k == DK - 1))
                ins.then_inc(router_done, 1)

            def rank(r):
                pe.wait_ge(mask_done, r + 1)
                pe.wait_ge(slots_done, r)
                mm(rank_ps[:, 0:NE], tri16[:], mask[:], start=True, stop=True)
                ins = mm(rank_ps[:, NE:2 * NE], ones16[:], mask[:], start=True, stop=True)
                if r == NT - 1:
                    v = N - r * P
                    ins = mm(rank_ps[:, 2 * NE:3 * NE], ones16[0:v, :], mask[0:v, :], start=True, stop=True)
                ins.then_inc(rank_done, 1)

            def turn_first(j, tiles):
                for i in tiles:
                    if j == 0:
                        pe.wait_ge(gathered[i], 16)
                    for h in range(2):
                        ins = mm(x4_ps[j % 2][:, i * P:(i + 1) * P],
                                 gx0[i].bitcast(F16)[:, h * D + j * P:h * D + (j + 1) * P],
                                 ident16[:], start=(h == 0), stop=(h == 1), skip_group_check=True)
                return ins

            pe.wait_ge(count_lo_done, NT)
            for r in range(NT + 2):
                if r < NT:
                    aggregate(r, 0)
                if r >= 2:
                    route(r - 2)
                if r < NT:
                    aggregate(r, 1)
                if 1 <= r <= NT:
                    turn2(r - 1)
                if r == NT + 1:
                    for j in range(2):
                        turn_first(j, FIRST).then_inc(first_done, 1)
                if r >= 2:
                    rank(r - 2)

            pe.sem_inc(down_done, 1)

            def turn4(c, j):
                pe.wait_ge(x4_lo_done, c * DK + (j + 1))
                for i in range(CT):
                    if j == 0:
                        pe.wait_ge(gathered[i], c * 16 + 16)
                    for h in range(2):
                        ins = mm(x4_ps[j % 2][:, i * P:(i + 1) * P],
                                 gx[i].bitcast(F16)[:, h * D + j * P:h * D + (j + 1) * P],
                                 ident16[:], start=(h == 0), stop=(h == 1), skip_group_check=True)
                ins.then_inc(x4_done, 1)

            def up(c, w_hi, w_lo, wide=CH, first=0):
                together = 3 if first else 2
                for js in [(j,) for j in range(DK - together)] + [tuple(range(DK - together, DK))]:
                    for j in js:
                        pe.wait_ge(x4_lo_done, c * DK + (j + 3))
                        if first and j + 2 < DK:
                            turn_first(j + 2, range(len(FIRST), CT)).then_inc(x4_done, 1)
                    for f in range(FK):
                        for j in js:
                            ws = slice(j * FF + f * P, j * FF + (f + 1) * P)
                            x_hi, x_lo = [x4[:, at + first:at + wide] for at in (2 * j * CH, (2 * j + 1) * CH)]
                            o = up_ps[f][:, first:wide]
                            mm(o, w_hi[:, ws], x_hi, start=(j == 0), stop=False)
                            mm(o, w_hi[:, ws], x_lo, start=False, stop=False)
                            ins = mm(o, w_lo[:, ws], x_hi, start=False, stop=(j == DK - 1))
                        if js[-1] == DK - 1:
                            ins.then_inc(up_done, 1)

            def down(c, w_hi, w_lo, last=False):
                if not last:
                    turn4(c + 1, 0)
                    turn4(c + 1, 1)
                for i in range(CT):
                    for n in range(2):
                        k = 2 * i + n
                        pe.wait_ge(down_read, c * (2 * CT) + (k + 1))
                        for f in range(FK):
                            if k == 0:
                                pe.wait_ge(y_lo_done, c * FK + (f + 1))
                            ys = slice(f * CH + i * P, f * CH + (i + 1) * P)
                            ws = slice(W2AT + f * D + n * HALF, W2AT + f * D + (n + 1) * HALF)
                            mm(down_ps[n], y_hi[:, ys], w_hi[:, ws], start=(f == 0), stop=False)
                            mm(down_ps[n], y_hi[:, ys], w_lo[:, ws], start=False, stop=False)
                            ins = mm(down_ps[n], y_lo[:, ys], w_hi[:, ws], start=False, stop=(f == FK - 1))
                        ins.then_inc(down_done, 1)
                        if not last:
                            turn4(c + 1, k + 2)

            def chunk(c, e, h, width=None, last=False):
                pe.wait_ge(gelu_done, c * FK + FK)
                if width is None:
                    up(c, e_hi[h], e_lo[h])
                else:
                    for k, wide in enumerate(WIDTHS):
                        with pe.If(width == k):
                            up(c, e_hi[h], e_lo[h], wide)
                if not isinstance(e, int) or e:
                    pe.wait_ge(e_lo_done, e * PIECES)
                down(c, e_hi[h], e_lo[h], last)

            def expert(e, h):
                plan = pe.value_load(plans[0:1, ds(e, 1)], min_val=0, max_val=PLAN ** 2 * 4 - 1)
                c0, c1, width = plan // (4 * PLAN), plan // 4 % PLAN, plan % 4
                pe.wait_ge(e_lo_done, e * PIECES - FK)
                settle(pe)
                if isinstance(e, int) and e == NE - 1:
                    c_last = pe.value_load(last_chunk[:], min_val=NE - 1, max_val=MAXC - 3)
                    with pe.If(c_last > c0):
                        with pe.Fori(c0, c_last) as c:
                            chunk(c, e, h, width)
                    chunk(c_last, e, h, width, True)
                else:
                    with pe.Fori(c0, c1) as c:
                        chunk(c, e, h, width)

            pe.wait_ge(w_lo_done, 2 * PIECES)
            for j in range(DK):
                pe.wait_ge(first_lo_done, j + 1)
                for f in range(FK):
                    ws = slice(j * FF + f * P, j * FF + (f + 1) * P)
                    x_hi, x_lo = [x4[:, at:at + FIRST_CH] for at in (2 * j * CH, (2 * j + 1) * CH)]
                    o = up_ps[f][:, 0:FIRST_CH]
                    mm(o, e_hi[0][:, ws], x_hi, start=(j == 0), stop=False, skip_group_check=True)
                    mm(o, e_hi[0][:, ws], x_lo, start=False, stop=False, skip_group_check=True)
                    mm(o, e_lo[0][:, ws], x_hi, start=False, stop=(j == DK - 1), skip_group_check=True)
                if j + 2 < DK:
                    turn_first(j + 2, FIRST).then_inc(first_done, 1)
            pe.wait_ge(slots_done, NT)
            for j in range(2):
                turn_first(j, range(len(FIRST), CT)).then_inc(x4_done, 1)
            up(0, e_hi[0], e_lo[0], first=FIRST_CH)
            down(0, e_hi[0], e_lo[0])
            pe.wait_ge(ranges2_done, 1)
            pe.wait_ge(plans_done, 1)
            more = pe.value_load(ranges2[0:1, 3, 0:1], min_val=0, max_val=1)
            end = pe.value_load(ranges2[0:1, 1, 0:1], min_val=1, max_val=MAXC - 2)
            with pe.If(more):
                with pe.Fori(1, end) as c:
                    chunk(c, 0, 0)
            expert(1, 1)
            with pe.Fori(1, NE // 2 - 1) as pair:
                for h in range(2):
                    expert(pair * 2 + h, h)
            expert(NE - 2, 0)
            expert(NE - 1, 1)


def kernel(x, src, dst, L0_gnn_W, L0_gnn_b, L0_ffn_router_w, L0_ffn_router_b, L0_ffn_w1, L0_ffn_b1, L0_ffn_w2,
           L0_ffn_b2, L0_ffn_ln_w, L0_ffn_ln_b):
    import numpy as np
    import concourse.bacc as bacc
    from concourse.bass_utils import run_bass_kernel_spmd

    x = np.asarray(x)
    xp = np.zeros((NP, D), np.float32)
    xp[:N] = x
    src, dst = np.asarray(src), np.asarray(dst)

    def edge_tiles(a, behind):
        rows = np.full((ET * EP,), behind, a.dtype)
        rows[:E] = a
        return rows.reshape(ET, EP)

    wst = np.zeros((NE + 1, PIECES, P, D), np.float32)
    wst[0] = np.asarray(L0_gnn_W).T.reshape(PIECES, P, D)
    w1 = np.asarray(L0_ffn_w1).transpose(0, 2, 1).reshape(NE, DK // 2, 2, P, FF)
    wst[1:, :DK // 2] = w1.transpose(0, 1, 3, 2, 4).reshape(NE, DK // 2, P, D)
    wst[1:, DK // 2:] = np.asarray(L0_ffn_w2).transpose(0, 2, 1).reshape(NE, FK, P, D)
    arrays = {
        "x": xp,
        "src": np.ascontiguousarray(edge_tiles(src, -1).T),
        "dst": np.ascontiguousarray(edge_tiles(dst, -1).T),
        "dst_rows": edge_tiles(dst, dst[E - 1]),
        "wst": wst,
        "b": np.ascontiguousarray(np.asarray(L0_gnn_b)),
        "router_w": np.ascontiguousarray(np.asarray(L0_ffn_router_w).reshape(NE, DK, P).transpose(2, 1, 0)
                                         .reshape(P, DK * NE)),
        "router_b": np.ascontiguousarray(np.asarray(L0_ffn_router_b)),
        "b1": np.ascontiguousarray(np.asarray(L0_ffn_b1).reshape(NE * FK, P).T),
        "b2": np.ascontiguousarray(np.asarray(L0_ffn_b2)),
        "ln_w": np.ascontiguousarray(np.asarray(L0_ffn_ln_w)),
        "ln_b": np.ascontiguousarray(np.asarray(L0_ffn_ln_b)),
    }
    nc = bacc.Bacc("TRN2", target_bir_lowering=False, num_devices=1)
    args = {k: nc.dram_tensor(k + "_in", a.shape, mybir.dt.from_np(a.dtype), kind="ExternalInput").ap()
            for k, a in arrays.items()}
    y = nc.dram_tensor("out_dram", (NP, D), F32, kind="ExternalOutput").ap()
    scratch = {
        "x2_rows": nc.dram_tensor("x2_rows", (NROW, D), F32).ap(),
        "cw_rows": nc.dram_tensor("cw_rows", (NROW, NE), F32).ap(),
        "acc_rows": nc.dram_tensor("acc_rows", (NROW, D), F32).ap(),
        "slot_table": nc.dram_tensor("slot_table", (NE * CAP, 1), I32).ap(),
    }
    build(nc, **args, **scratch, out=y)
    r = run_bass_kernel_spmd(nc, [{k + "_in": a for k, a in arrays.items()}], core_ids=[0])
    return r.results[0]["out_dram"][:N]
```
